# Optimizing a Trainium2 kernel written in Bass

```python
import numpy as np
import jax
import jax.numpy as jnp

def _softmax(x, axis=-1):
    return jax.nn.softmax(x, axis=axis)

def _gelu(x):
    return jax.nn.gelu(x, approximate=True)

def _silu(x):
    return jax.nn.silu(x)

def _sigmoid(x):
    return jax.nn.sigmoid(x)

def _layernorm(x, axis=-1, eps=1e-05):
    m = jnp.mean(x, axis=axis, keepdims=True)
    v = jnp.var(x, axis=axis, keepdims=True)
    return (x - m) / jnp.sqrt(v + eps)

def _scatter_add(tgt, idx, src, axis=0):
    return tgt.at[idx].add(src)

def _segment_sum(src, seg, n):
    return jax.ops.segment_sum(src, seg, n)
kernel_name = 'mk_dlrm_tower_d1_rec_r8_3773d4'

def setup_inputs(seed: int=0):
    np.random.seed(seed)
    _w = jnp.asarray

    def _rec_inputs():
        import jax
        import jax.numpy as jnp
        _tk = jax.random.key(seed)
        dense_ctx = jax.random.normal(jax.random.fold_in(_tk, 190), (512, 16), jnp.float32)
        ids = jnp.stack([jax.random.randint(jax.random.fold_in(_tk, 200 + f), (512,), 0, v, jnp.int32) for f, v in enumerate([125000, 12500, 1000, 125000, 1250, 12500, 1000, 1000, 125000, 1250, 1000, 12500, 12500, 1000, 12500, 125000, 1250, 12500, 1000, 125000, 1000, 12500, 1000, 1250, 1000, 1250, 1250, 12500, 1000, 1250, 1250, 1250, 125000, 1000, 125000, 125000, 1250, 125000, 125000])], axis=1)
        tbl_0 = 0.05 * jax.random.normal(jax.random.fold_in(_tk, 500 + 0), (125000, 16), jnp.float32)
        tbl_1 = 0.05 * jax.random.normal(jax.random.fold_in(_tk, 500 + 1), (12500, 16), jnp.float32)
        tbl_2 = 0.05 * jax.random.normal(jax.random.fold_in(_tk, 500 + 2), (1000, 16), jnp.float32)
        tbl_3 = 0.05 * jax.random.normal(jax.random.fold_in(_tk, 500 + 3), (125000, 16), jnp.float32)
        tbl_4 = 0.05 * jax.random.normal(jax.random.fold_in(_tk, 500 + 4), (1250, 16), jnp.float32)
        tbl_5 = 0.05 * jax.random.normal(jax.random.fold_in(_tk, 500 + 5), (12500, 16), jnp.float32)
        tbl_6 = 0.05 * jax.random.normal(jax.random.fold_in(_tk, 500 + 6), (1000, 16), jnp.float32)
        tbl_7 = 0.05 * jax.random.normal(jax.random.fold_in(_tk, 500 + 7), (1000, 16), jnp.float32)
        tbl_8 = 0.05 * jax.random.normal(jax.random.fold_in(_tk, 500 + 8), (125000, 16), jnp.float32)
        tbl_9 = 0.05 * jax.random.normal(jax.random.fold_in(_tk, 500 + 9), (1250, 16), jnp.float32)
        tbl_10 = 0.05 * jax.random.normal(jax.random.fold_in(_tk, 500 + 10), (1000, 16), jnp.float32)
        tbl_11 = 0.05 * jax.random.normal(jax.random.fold_in(_tk, 500 + 11), (12500, 16), jnp.float32)
        tbl_12 = 0.05 * jax.random.normal(jax.random.fold_in(_tk, 500 + 12), (12500, 16), jnp.float32)
        tbl_13 = 0.05 * jax.random.normal(jax.random.fold_in(_tk, 500 + 13), (1000, 16), jnp.float32)
        tbl_14 = 0.05 * jax.random.normal(jax.random.fold_in(_tk, 500 + 14), (12500, 16), jnp.float32)
        tbl_15 = 0.05 * jax.random.normal(jax.random.fold_in(_tk, 500 + 15), (125000, 16), jnp.float32)
        tbl_16 = 0.05 * jax.random.normal(jax.random.fold_in(_tk, 500 + 16), (1250, 16), jnp.float32)
        tbl_17 = 0.05 * jax.random.normal(jax.random.fold_in(_tk, 500 + 17), (12500, 16), jnp.float32)
        tbl_18 = 0.05 * jax.random.normal(jax.random.fold_in(_tk, 500 + 18), (1000, 16), jnp.float32)
        tbl_19 = 0.05 * jax.random.normal(jax.random.fold_in(_tk, 500 + 19), (125000, 16), jnp.float32)
        tbl_20 = 0.05 * jax.random.normal(jax.random.fold_in(_tk, 500 + 20), (1000, 16), jnp.float32)
        tbl_21 = 0.05 * jax.random.normal(jax.random.fold_in(_tk, 500 + 21), (12500, 16), jnp.float32)
        tbl_22 = 0.05 * jax.random.normal(jax.random.fold_in(_tk, 500 + 22), (1000, 16), jnp.float32)
        tbl_23 = 0.05 * jax.random.normal(jax.random.fold_in(_tk, 500 + 23), (1250, 16), jnp.float32)
        tbl_24 = 0.05 * jax.random.normal(jax.random.fold_in(_tk, 500 + 24), (1000, 16), jnp.float32)
        tbl_25 = 0.05 * jax.random.normal(jax.random.fold_in(_tk, 500 + 25), (1250, 16), jnp.float32)
        tbl_26 = 0.05 * jax.random.normal(jax.random.fold_in(_tk, 500 + 26), (1250, 16), jnp.float32)
        tbl_27 = 0.05 * jax.random.normal(jax.random.fold_in(_tk, 500 + 27), (12500, 16), jnp.float32)
        tbl_28 = 0.05 * jax.random.normal(jax.random.fold_in(_tk, 500 + 28), (1000, 16), jnp.float32)
        tbl_29 = 0.05 * jax.random.normal(jax.random.fold_in(_tk, 500 + 29), (1250, 16), jnp.float32)
        tbl_30 = 0.05 * jax.random.normal(jax.random.fold_in(_tk, 500 + 30), (1250, 16), jnp.float32)
        tbl_31 = 0.05 * jax.random.normal(jax.random.fold_in(_tk, 500 + 31), (1250, 16), jnp.float32)
        tbl_32 = 0.05 * jax.random.normal(jax.random.fold_in(_tk, 500 + 32), (125000, 16), jnp.float32)
        tbl_33 = 0.05 * jax.random.normal(jax.random.fold_in(_tk, 500 + 33), (1000, 16), jnp.float32)
        tbl_34 = 0.05 * jax.random.normal(jax.random.fold_in(_tk, 500 + 34), (125000, 16), jnp.float32)
        tbl_35 = 0.05 * jax.random.normal(jax.random.fold_in(_tk, 500 + 35), (125000, 16), jnp.float32)
        tbl_36 = 0.05 * jax.random.normal(jax.random.fold_in(_tk, 500 + 36), (1250, 16), jnp.float32)
        tbl_37 = 0.05 * jax.random.normal(jax.random.fold_in(_tk, 500 + 37), (125000, 16), jnp.float32)
        tbl_38 = 0.05 * jax.random.normal(jax.random.fold_in(_tk, 500 + 38), (125000, 16), jnp.float32)
        _rk = jax.random.fold_in(_tk, 7)
        W_top1 = 0.0402911 * jax.random.normal(jax.random.fold_in(_tk, 801), (616, 512), jnp.float32)
        W_top2 = 0.0441942 * jax.random.normal(jax.random.fold_in(_tk, 802), (512, 256), jnp.float32)
        W_top3 = 0.0625 * jax.random.normal(jax.random.fold_in(_tk, 803), (256, 1), jnp.float32)
        b_top1 = jnp.zeros((512,), jnp.float32)
        b_top2 = jnp.zeros((256,), jnp.float32)
        return (dense_ctx, ids, tbl_0, tbl_1, tbl_2, tbl_3, tbl_4, tbl_5, tbl_6, tbl_7, tbl_8, tbl_9, tbl_10, tbl_11, tbl_12, tbl_13, tbl_14, tbl_15, tbl_16, tbl_17, tbl_18, tbl_19, tbl_20, tbl_21, tbl_22, tbl_23, tbl_24, tbl_25, tbl_26, tbl_27, tbl_28, tbl_29, tbl_30, tbl_31, tbl_32, tbl_33, tbl_34, tbl_35, tbl_36, tbl_37, tbl_38, W_top1, b_top1, W_top2, b_top2, W_top3)
    dense_ctx, ids, tbl_0, tbl_1, tbl_2, tbl_3, tbl_4, tbl_5, tbl_6, tbl_7, tbl_8, tbl_9, tbl_10, tbl_11, tbl_12, tbl_13, tbl_14, tbl_15, tbl_16, tbl_17, tbl_18, tbl_19, tbl_20, tbl_21, tbl_22, tbl_23, tbl_24, tbl_25, tbl_26, tbl_27, tbl_28, tbl_29, tbl_30, tbl_31, tbl_32, tbl_33, tbl_34, tbl_35, tbl_36, tbl_37, tbl_38, W_top1, b_top1, W_top2, b_top2, W_top3 = _rec_inputs()

    def _L0_rec_setup():
        import jax, jax.numpy as jnp
        import numpy as np
        B, F0, D = (256, 39, 16)
        CROSS = [200, 200, 200]
        key = jax.random.key(seed)
        ks = jax.random.split(key, 7)
        inp = {'x': jax.random.normal(ks[0], (B, F0, D), dtype=jnp.float32)}
        prev = F0
        for i, c in enumerate(CROSS):
            scale = 1.0 / np.sqrt(F0 * prev)
            inp[f'W{i}'] = jax.random.normal(ks[1 + 2 * i], (c, F0, prev), dtype=jnp.float32) * scale
            inp[f'b{i}'] = jnp.zeros((c,), dtype=jnp.float32)
            prev = c
        return inp
    _L0_rec_all = _L0_rec_setup()
    _L0_rec_in = {k: v for k, v in _L0_rec_all.items() if k in ('W0', 'b0', 'W1', 'b1', 'W2', 'b2')}
    del _L0_rec_all
    return {'dense_ctx': dense_ctx, 'ids': ids, 'tbl_0': tbl_0, 'tbl_1': tbl_1, 'tbl_2': tbl_2, 'tbl_3': tbl_3, 'tbl_4': tbl_4, 'tbl_5': tbl_5, 'tbl_6': tbl_6, 'tbl_7': tbl_7, 'tbl_8': tbl_8, 'tbl_9': tbl_9, 'tbl_10': tbl_10, 'tbl_11': tbl_11, 'tbl_12': tbl_12, 'tbl_13': tbl_13, 'tbl_14': tbl_14, 'tbl_15': tbl_15, 'tbl_16': tbl_16, 'tbl_17': tbl_17, 'tbl_18': tbl_18, 'tbl_19': tbl_19, 'tbl_20': tbl_20, 'tbl_21': tbl_21, 'tbl_22': tbl_22, 'tbl_23': tbl_23, 'tbl_24': tbl_24, 'tbl_25': tbl_25, 'tbl_26': tbl_26, 'tbl_27': tbl_27, 'tbl_28': tbl_28, 'tbl_29': tbl_29, 'tbl_30': tbl_30, 'tbl_31': tbl_31, 'tbl_32': tbl_32, 'tbl_33': tbl_33, 'tbl_34': tbl_34, 'tbl_35': tbl_35, 'tbl_36': tbl_36, 'tbl_37': tbl_37, 'tbl_38': tbl_38, 'W_top1': W_top1, 'b_top1': b_top1, 'W_top2': W_top2, 'b_top2': b_top2, 'W_top3': W_top3, 'L0_rec_W0': _L0_rec_in['W0'], 'L0_rec_b0': _L0_rec_in['b0'], 'L0_rec_W1': _L0_rec_in['W1'], 'L0_rec_b1': _L0_rec_in['b1'], 'L0_rec_W2': _L0_rec_in['W2'], 'L0_rec_b2': _L0_rec_in['b2']}

def reference(dense_ctx, ids, tbl_0, tbl_1, tbl_2, tbl_3, tbl_4, tbl_5, tbl_6, tbl_7, tbl_8, tbl_9, tbl_10, tbl_11, tbl_12, tbl_13, tbl_14, tbl_15, tbl_16, tbl_17, tbl_18, tbl_19, tbl_20, tbl_21, tbl_22, tbl_23, tbl_24, tbl_25, tbl_26, tbl_27, tbl_28, tbl_29, tbl_30, tbl_31, tbl_32, tbl_33, tbl_34, tbl_35, tbl_36, tbl_37, tbl_38, W_top1, b_top1, W_top2, b_top2, W_top3, L0_rec_W0, L0_rec_b0, L0_rec_W1, L0_rec_b1, L0_rec_W2, L0_rec_b2):
    import jax
    import jax.numpy as jnp

    def _L0_rec_ref(x, W0, b0, W1, b1, W2, b2):
        import jax, jax.numpy as jnp
        import numpy as np
        B, F0, D = (256, 39, 16)
        CROSS = [200, 200, 200]
        x0 = x
        h = x
        xs = []
        for W, b in ((W0, b0), (W1, b1), (W2, b2)):
            z = jnp.einsum('bfd,bgd,ofg->bod', x0, h, W) + b[None, :, None]
            h = jax.nn.relu(z)
            xs.append(h)
        return jnp.sum(jnp.concatenate(xs, axis=1), axis=2)
    e = jnp.stack([tbl_0[ids[:, 0]], tbl_1[ids[:, 1]], tbl_2[ids[:, 2]], tbl_3[ids[:, 3]], tbl_4[ids[:, 4]], tbl_5[ids[:, 5]], tbl_6[ids[:, 6]], tbl_7[ids[:, 7]], tbl_8[ids[:, 8]], tbl_9[ids[:, 9]], tbl_10[ids[:, 10]], tbl_11[ids[:, 11]], tbl_12[ids[:, 12]], tbl_13[ids[:, 13]], tbl_14[ids[:, 14]], tbl_15[ids[:, 15]], tbl_16[ids[:, 16]], tbl_17[ids[:, 17]], tbl_18[ids[:, 18]], tbl_19[ids[:, 19]], tbl_20[ids[:, 20]], tbl_21[ids[:, 21]], tbl_22[ids[:, 22]], tbl_23[ids[:, 23]], tbl_24[ids[:, 24]], tbl_25[ids[:, 25]], tbl_26[ids[:, 26]], tbl_27[ids[:, 27]], tbl_28[ids[:, 28]], tbl_29[ids[:, 29]], tbl_30[ids[:, 30]], tbl_31[ids[:, 31]], tbl_32[ids[:, 32]], tbl_33[ids[:, 33]], tbl_34[ids[:, 34]], tbl_35[ids[:, 35]], tbl_36[ids[:, 36]], tbl_37[ids[:, 37]], tbl_38[ids[:, 38]]], axis=1)
    z = _L0_rec_ref(e, L0_rec_W0, L0_rec_b0, L0_rec_W1, L0_rec_b1, L0_rec_W2, L0_rec_b2)
    z = z.reshape(z.shape[0], -1)
    h = jnp.concatenate([z, dense_ctx], axis=1)
    h = jnp.maximum(h @ W_top1 + b_top1, 0.0)
    h = jnp.maximum(h @ W_top2 + b_top2, 0.0)
    y = h @ W_top3
    return y

_drawn_inputs = setup_inputs


def setup_inputs(seed=0):
    import zlib

    import numpy as np

    out = dict(_drawn_inputs(seed))
    spreads = {'b_top1': (0.0, 0.8),
     'b_top2': (0.0, 0.299),
     'L0_rec_b0': (0.0, 0.1),
     'L0_rec_b1': (0.0, 0.1),
     'L0_rec_b2': (0.0, 0.28)}
    factors = {'tbl_0': 8.0,
     'tbl_1': 8.0,
     'tbl_2': 8.0,
     'tbl_3': 8.0,
     'tbl_4': 8.0,
     'tbl_5': 8.0,
     'tbl_6': 8.0,
     'tbl_7': 8.0,
     'tbl_8': 8.0,
     'tbl_9': 8.0,
     'tbl_10': 8.0,
     'tbl_11': 8.0,
     'tbl_12': 8.0,
     'tbl_13': 8.0,
     'tbl_14': 8.0,
     'tbl_15': 8.0,
     'tbl_16': 8.0,
     'tbl_17': 8.0,
     'tbl_18': 8.0,
     'tbl_19': 8.0,
     'tbl_20': 8.0,
     'tbl_21': 8.0,
     'tbl_22': 8.0,
     'tbl_23': 8.0,
     'tbl_24': 8.0,
     'tbl_25': 8.0,
     'tbl_26': 8.0,
     'tbl_27': 8.0,
     'tbl_28': 8.0,
     'tbl_29': 8.0,
     'tbl_30': 8.0,
     'tbl_31': 8.0,
     'tbl_32': 8.0,
     'tbl_33': 8.0,
     'tbl_34': 8.0,
     'tbl_35': 8.0,
     'tbl_36': 8.0,
     'tbl_37': 8.0,
     'tbl_38': 8.0,
     'L0_rec_W0': 8.0,
     'L0_rec_W1': 7.689,
     'L0_rec_W2': 7.744,
     'dense_ctx': 3.609}
    for name, (base, spread) in spreads.items():
        noise = np.random.default_rng([zlib.crc32(name.encode()), seed]).standard_normal(out[name].shape)
        drawn = base * np.exp(spread * noise) if base else spread * noise
        out[name] = jnp.asarray(drawn.astype(out[name].dtype))
    for name, factor in factors.items():
        out[name] = (out[name] * factor).astype(out[name].dtype)
    return out
```

```python
import concourse.bass as bass
from concourse import mybir
from contextlib import ExitStack

P = 128
B = 512
F = 39
D = 16
O = 200
NBLK = B // P
NCH = NBLK * D
K2 = F // 2 + 1
FE = F + K2 - 1
KT = 3
T0 = -(-K2 // KT)
R0 = KT * F
NPAIR = K2 * F
GA = 128
GB = O - GA
GH = GB // 2
RS = GB + GH
NG = (F + 1) // 2
NBANK = 4
SCOL = 2 * (GA + RS)
TOP_IN = 3 * O + 16
M1, M2 = 512, 256
KT1 = -(-TOP_IN // P)


def group_cols(g):
    return min(2, F - 2 * g) * O


def dlrm_tower(nc, ids, tables, dense, w0_a, w0_b, w1, w2, b0, b1, b2, wt1, bt1, wt2, bt2, wt3, out):
    f32, f32r, i32 = mybir.dt.float32, mybir.dt.float32r, mybir.dt.int32
    ALU, ACT = mybir.AluOpType, mybir.ActivationFunctionType
    z1_dram = nc.dram_tensor("z1_between_phases", (NCH, P, O), f32, kind="Internal").ap()

    ctx = ExitStack()
    with ctx:
        def sb(name, shape, dt=f32):
            return ctx.enter_context(nc.sbuf_tensor(name, shape, dt))

        def pb(name, shape):
            return ctx.enter_context(nc.psum_tensor(name, shape, f32))

        def sem(name):
            return ctx.enter_context(nc.semaphore(name))

        w_hi = sb("w_hi", [GA, F * O], f32r)
        w_lo = sb("w_lo", [GA, F * O], f32r)
        w_st = sb("w_st", [P, 2, F * O], f32r)
        n_prod, n_stage, n_gath, n_x0 = 2 * T0 * R0, 2 * 3 * 2 * O, 2 * F * D, NCH * FE
        area = sb("area", [P, n_prod + n_stage + n_gath + n_x0])
        prod = area[:, 0:n_prod].rearrange("p (u n) -> p u n", u=2)
        stage = area[:, n_prod:n_prod + n_stage].rearrange("p (u s n) -> p u s n", u=2, s=3)
        at = n_prod + n_stage
        gath = area[:, at:at + n_gath].rearrange("p (u f d) -> p u f d", u=2, d=D)
        x0_all = area[:, at + n_gath:at + n_gath + n_x0].rearrange("p (c f) -> p c f", f=FE)
        assert KT1 * M1 + 4 * M2 <= n_prod + n_stage
        wt1_sb = area[:, 0:KT1 * M1].rearrange("p (t n) -> p t n", n=M1)
        wt2_sb = area[:, KT1 * M1:KT1 * M1 + 4 * M2].rearrange("p (t n) -> p t n", n=M2)
        assert (KT1 + 4) * B <= n_gath + n_x0
        xT = area[:, at:at + KT1 * B].rearrange("p (t n) -> p t n", n=B)
        h1T = area[:, at + KT1 * B:at + (KT1 + 4) * B].rearrange("p (t n) -> p t n", n=B)
        h2T = area[:, at:at + 2 * B].rearrange("p (t n) -> p t n", n=B)
        y_sb = area[0:1, at + 2 * B:at + 3 * B]

        stack_hi = sb("stack_hi", [P, 2, 2 * O])
        w0_hi = sb("w0_hi", [R0, T0, O], f32r)
        w0_lo = sb("w0_lo", [R0, T0, O], f32r)
        prodT_hi = sb("prodT_hi", [R0, T0, P], f32r)
        prodT_lo = sb("prodT_lo", [R0, T0, P], f32r)
        top_x = sb("top_x", [P, NBLK, TOP_IN])
        hs = sb("hs", [P, SCOL], f32r)
        hT = sb("hT", [P, 2, 4, P], f32r)
        z0_sb = sb("z0_sb", [P, O])
        z1_out = sb("z1_out", [P, 2, O])
        z1_in = sb("z1_in", [P, 2, O])
        z2_sb = sb("z2_sb", [P, 2, O])
        acc = sb("acc", [P, 2, 2, O])
        x0 = sb("x0", [P, 2, F])
        bias = sb("bias", [P, 3, O])
        ids_sb = sb("ids_sb", [P, NBLK, F], i32)
        ident = sb("ident", [P, P])
        minus_lo_rows = sb("minus_lo_rows", [P, 1])
        bt1_sb = sb("bt1_sb", [P, 4])
        bt2_sb = sb("bt2_sb", [P, 2])
        wt3_sb = sb("wt3_sb", [P, 2])

        y_ps = pb("y_ps", [P, NBANK, 512])
        prodT_ps = pb("prodT_ps", [P, 8, P])
        z0_ps = pb("z0_ps", [P, 512])
        hT_ps = pb("hT_ps", [P, 4, P])

        ids_in = sem("ids_in")
        w0_in = sem("w0_in")
        small_in = sem("small_in")
        top_in = sem("top_in")
        raw_in = [sem(f"raw_in{u}") for u in range(2)]
        z1_loaded = [sem(f"z1_loaded{u}") for u in range(2)]
        z1_stored = [sem(f"z1_stored{u}") for u in range(2)]
        gathered = [sem(f"gathered{b}") for b in range(NBLK)]
        out_stored = sem("out_stored")
        blank = sem("blank")
        w0_blank = sem("w0_blank")
        consts = sem("consts")
        w0_sum = sem("w0_sum")
        w0_hi_done = sem("w0_hi_done")
        w0_done = sem("w0_done")
        top_blank = sem("top_blank")
        w_hi_done = sem("w_hi_done")
        w_done = sem("w_done")
        x0_block = sem("x0_block")
        x0_ready = sem("x0_ready")
        prod_ready = sem("prod_ready")
        prodT_done = sem("prodT_done")
        prodT_hi_done = sem("prodT_hi_done")
        prodT_lo_done = sem("prodT_lo_done")
        z0_done = sem("z0_done")
        z0_biased = sem("z0_biased")
        hs_hi = sem("hs_hi")
        hs_lo = sem("hs_lo")
        hT_done = sem("hT_done")
        hT_ready = sem("hT_ready")
        y_done = sem("y_done")
        summed = sem("summed")
        z_done = sem("z_done")
        sums0 = sem("sums0")
        sums12 = sem("sums12")
        xT_ps_done = sem("xT_ps_done")
        xT_done = sem("xT_done")
        top_mm = sem("top_mm")
        top_act = sem("top_act")

        block = ctx.enter_context(nc.Block())

        def wait(eng, s, count):
            if not isinstance(count, int) or count > 0:
                eng.wait_ge(s, count)

        def over_chunks(eng, step):
            step(0, 0, False)
            step(1, 1, False)
            with eng.Fori(1, NCH // 2 - 1) as i:
                step(2 * i, 0, False)
                step(2 * i + 1, 1, False)
            step(NCH - 2, 0, False)
            step(NCH - 1, 1, True)

        def fields_summed(c, g):
            return c * F + min(2 * g + 2, F)

        def bank_free(c, g):
            return fields_summed(c, g - NBANK) if g >= NBANK else fields_summed(c - 1, g - NBANK + NG)

        @block.sync
        def _(sp):
            sp.dma_start(ids_sb[:], ids.rearrange("(b p) f -> p b f", p=P)).then_inc(ids_in, 16)
            a_raw = area[:, 0:T0 * O].rearrange("p (t o) -> p t o", o=O)
            b_raw = top_x[:].rearrange("p b n -> p (b n)")[:, 0:T0 * O].rearrange("p (t o) -> p t o", o=O)
            full = (T0 - 1) * R0
            last = NPAIR - full
            sp.wait_ge(w0_blank, 2)
            sp.dma_start(a_raw[0:R0, 0:T0 - 1, :], w0_a[0:full, :].rearrange("(t p) o -> p t o", p=R0)).then_inc(w0_in, 16)
            sp.dma_start(a_raw[0:last, T0 - 1, :], w0_a[full:NPAIR, :]).then_inc(w0_in, 16)
            sp.dma_start(b_raw[F:R0, 0, :], w0_b[0:R0 - F, :]).then_inc(w0_in, 16)
            sp.dma_start(b_raw[0:R0, 1:T0 - 1, :], w0_b[R0 - F:full - F, :].rearrange("(t p) o -> p t o", p=R0)).then_inc(w0_in, 16)
            sp.dma_start(b_raw[0:last, T0 - 1, :], w0_b[full - F:NPAIR - F, :]).then_inc(w0_in, 16)

            def load_weights(w, layer):
                for g in range(NG):
                    n = layer * NG + g
                    cols = slice(2 * g * O, 2 * g * O + group_cols(g))
                    to = stage[:, n % 2, :, 0:group_cols(g)]
                    wait(sp, w_done, 2 * (n - 1))
                    sp.dma_start(to[:, 0, :], w[0:GA, cols]).then_inc(raw_in[n % 2], 16)
                    sp.dma_start(to[0:GB, 1, :], w[GA:O, cols]).then_inc(raw_in[n % 2], 16)
                    sp.dma_start(to[GB:RS, 1, :], w[GA:GA + GH, cols]).then_inc(raw_in[n % 2], 16)
                    sp.dma_start(to[0:GB, 2, :], w[GA:O, cols]).then_inc(raw_in[n % 2], 16)
                    sp.dma_start(to[GB:RS, 2, :], w[GA + GH:O, cols]).then_inc(raw_in[n % 2], 16)

            load_weights(w1, 0)

            def load_z1(c, u):
                wait(sp, hs_hi, 2 * (NCH + c - 1))
                wait(sp, hs_lo, NCH + c - 1)
                sp.dma_start(z1_in[:, u, :], z1_dram[c, :, :]).then_inc(z1_loaded[u], 16)

            def store_z1(c, u, last):
                sp.wait_ge(z_done, c + 1)
                sp.dma_start(z1_dram[c, :, :], z1_out[:, u, :]).then_inc(z1_stored[u], 16)

            over_chunks(sp, store_z1)
            for u in range(2):
                sp.wait_ge(z1_stored[u], 16 * NCH // 2)
            load_z1(0, 0)
            load_z1(1, 1)
            load_weights(w2, 1)
            sp.wait_ge(w_done, 4 * NG)
            full = (KT1 - 1) * P
            sp.dma_start(wt1_sb[:, 0:KT1 - 1, :], wt1[0:full, :].rearrange("(t p) n -> p t n", p=P)).then_inc(top_in, 16)
            sp.dma_start(wt1_sb[0:TOP_IN - full, KT1 - 1, :], wt1[full:TOP_IN, :]).then_inc(top_in, 16)
            sp.dma_start(wt2_sb, wt2.rearrange("(t p) n -> p t n", p=P)).then_inc(top_in, 16)
            with sp.Fori(1, NCH // 2) as i:
                load_z1(2 * i, 0)
                load_z1(2 * i + 1, 1)
            sp.wait_ge(top_act, 7)
            sp.dma_start(out.rearrange("b a -> a b"), y_sb).then_inc(out_stored, 16)
            sp.wait_ge(out_stored, 16)

        @block.gpsimd
        def _(pool):
            nc.gpsimd.memset(area[:, 0:T0 * O], 0.0).then_inc(w0_blank, 1)
            nc.gpsimd.memset(top_x[:], 0.0).then_inc(w0_blank, 1)
            nc.gpsimd.memset(ident[:], 0.0).then_inc(blank, 1)
            nc.gpsimd.memset(minus_lo_rows[:], 0.0).then_inc(blank, 1)
            pool.wait_ge(blank, 2)
            nc.gpsimd.affine_select(out=ident[:], in_=ident[:], compare_op=ALU.not_equal, fill=1.0, base=0,
                                    pattern=[[-1, P]], channel_multiplier=1).then_inc(consts, 1)
            nc.gpsimd.affine_select(out=minus_lo_rows[:], in_=minus_lo_rows[:], compare_op=ALU.is_ge, fill=-1.0,
                                    base=GB - 1, pattern=[[0, 1]], channel_multiplier=-1).then_inc(consts, 1)

            def gather(b, f):
                nc.gpsimd.indirect_dma_start(
                    gath[:, b % 2, f, :], None, tables[f],
                    bass.IndirectOffsetOnAxis(ap=ids_sb[:, b, f:f + 1], axis=0)).then_inc(gathered[b], 16)

            def chunk_major(b):
                pool.wait_ge(gathered[b], 16 * F)
                to = x0_all[:, b * D:(b + 1) * D, :]
                rows = gath[:, b % 2, :, :].rearrange("p f d -> p d f")
                nc.gpsimd.tensor_copy(to[:, :, 0:F], rows).then_inc(x0_block, 1)
                nc.gpsimd.tensor_copy(to[:, :, F:FE], rows[:, :, 0:FE - F]).then_inc(x0_block, 1)

            def products(c, u, blocks):
                row = x0_all[:, c, :]
                near = row[:, 0:F].unsqueeze(1).to_broadcast([P, K2, F])
                far = bass.AP(tensor=row.tensor, offset=row.offset, ap=[list(row.ap[0]), [1, K2], [1, F]])
                wait(pool, prodT_done, c - 1)
                pool.wait_ge(x0_block, 2 * blocks)
                nc.gpsimd.tensor_tensor(prod[:, u, 0:NPAIR].rearrange("p (k f) -> p k f", f=F), near, far,
                                        ALU.mult).then_inc(prod_ready, 1)

            pool.wait_ge(ids_in, 16)
            for f in range(F):
                gather(0, f)
            chunk_major(0)
            pool.wait_ge(w0_done, 1)
            for u in range(2):
                nc.gpsimd.memset(prod[:, u, NPAIR:T0 * R0], 0.0).then_inc(prod_ready, 1)
            per_chunk = -(-F // (D - 3))
            for b in range(NBLK - 1):
                for d in range(D):
                    products(b * D + d, d % 2, b + 1)
                    for f in range(per_chunk * d, min(per_chunk * (d + 1), F)):
                        gather(b + 1, f)
                chunk_major(b + 1)
            with pool.Fori(0, D // 2) as i:
                for u in range(2):
                    products((NBLK - 1) * D + 2 * i + u, u, NBLK)

        @block.scalar
        def _(act):
            for l, b in enumerate((b0, b1, b2)):
                act.dma_start(bias[:, l, :], b.rearrange("(a n) -> a n", a=1).to_broadcast([P, O])).then_inc(small_in, 16)
            act.dma_start(bt1_sb[:], bt1).then_inc(small_in, 16)
            act.dma_start(bt2_sb[:], bt2).then_inc(small_in, 16)
            act.dma_start(wt3_sb[:], wt3).then_inc(small_in, 16)
            act.wait_ge(top_blank, 1)
            act.dma_start(top_x[:, :, 3 * O:TOP_IN], dense.rearrange("(b p) n -> p b n", p=P)).then_inc(small_in, 16)

            act.wait_ge(w0_sum, 1)
            nc.scalar.activation(w0_hi[:], area[0:R0, 0:T0 * O].rearrange("p (t o) -> p t o", o=O),
                                 ACT.Copy).then_inc(w0_hi_done, 1)

            def round_weights(layer):
                for g in range(NG):
                    n = layer * NG + g
                    size = group_cols(g)
                    cols = slice(2 * g * O, 2 * g * O + size)
                    act.wait_ge(raw_in[n % 2], 16 * 5 * (n // 2 + 1))
                    if layer:
                        act.wait_ge(y_done, (NCH - 1) * NG + g + 1)
                    nc.scalar.activation(w_hi[:, cols], stage[:, n % 2, 0, 0:size], ACT.Copy).then_inc(w_hi_done, 1)
                    wait(act, w_done, 2 * n)
                    nc.scalar.activation(stack_hi[0:RS, :, 0:size].bitcast(f32r), stage[0:RS, n % 2, 1:3, 0:size],
                                         ACT.Copy).then_inc(w_hi_done, 1)

            def hidden_hi(z, n):
                wait(act, hT_done, n)
                nc.scalar.activation(hs[:, 0:O], z, ACT.Relu).then_inc(hs_hi, 1)
                twice = hs[:].rearrange("p (a n) -> p a n", a=2)[:, :, O:O + GH]
                nc.scalar.activation(twice, z[:, GA:O].rearrange("p (a n) -> p a n", a=2), ACT.Relu).then_inc(hs_hi, 1)

            def hidden_T(n, u, groups):
                act.wait_ge(hT_done, n + 1)
                wait(act, y_done, groups)
                nc.scalar.activation(hT[:, u, 0:2, :], hT_ps[:, 0:2, :], ACT.Copy).then_inc(hT_ready, 1)
                nc.scalar.activation(hT[0:RS, u, 2:4, :], hT_ps[0:RS, 2:4, :], ACT.Copy).then_inc(hT_ready, 1)

            def prepare1(c, u):
                act.wait_ge(prodT_done, c + 1)
                wait(act, z0_done, c)
                nc.scalar.activation(prodT_hi[:], prodT_ps[0:R0, 0:T0, :], ACT.Copy).then_inc(prodT_hi_done, 1)
                act.wait_ge(z0_biased, c + 1)
                hidden_hi(z0_sb[:], c)
                hidden_T(c, u, NG * (c - 1))

            def prepare2(c, u):
                act.wait_ge(z1_loaded[u], z1_count(c, u))
                hidden_hi(z1_in[:, u, :], NCH + c)
                hidden_T(NCH + c, u, NG * (NCH + c - 1))

            def z1_count(c, u):
                return 8 * (c - u) + 16

            round_weights(0)
            prepare1(0, 0)
            over_chunks(act, lambda c, u, last: None if last else prepare1(c + 1, 1 - u))
            round_weights(1)
            prepare2(0, 0)
            over_chunks(act, lambda c, u, last: None if last else prepare2(c + 1, 1 - u))

            act.wait_ge(xT_ps_done, 1)
            nc.scalar.activation(xT[:, 0:2, :], y_ps[:, 0:2, :], ACT.Copy).then_inc(xT_done, 1)
            for m in range(4):
                act.wait_ge(top_mm, m + 1)
                nc.scalar.activation(h1T[:, m, :], y_ps[:, m, :], ACT.Relu, bias=bt1_sb[:, m:m + 1]).then_inc(top_act, 1)
            two = prodT_ps[:].rearrange("p (t a) n -> p t (a n)", t=2)
            for m in range(2):
                act.wait_ge(top_mm, 5 + m)
                nc.scalar.activation(h2T[:, m, :], two[:, m, :], ACT.Relu, bias=bt2_sb[:, m:m + 1]).then_inc(top_act, 1)
            act.wait_ge(top_mm, 7)
            nc.scalar.activation(y_sb, z0_ps[0:1, 0:B], ACT.Copy).then_inc(top_act, 1)

        @block.vector
        def _(dve):
            a_raw = area[0:R0, 0:T0 * O]
            b_raw = top_x[:].rearrange("p b n -> p (b n)")[0:R0, 0:T0 * O]
            dve.wait_ge(w0_in, 5 * 16)
            nc.vector.tensor_tensor(a_raw, a_raw, b_raw, ALU.add).then_inc(w0_sum, 1)
            dve.wait_ge(w0_sum, 1)
            nc.vector.memset(top_x[:], 0.0).then_inc(top_blank, 1)
            dve.wait_ge(w0_hi_done, 1)
            nc.vector.tensor_tensor(w0_lo[:].rearrange("p t o -> p (t o)"), a_raw,
                                    w0_hi[:].bitcast(f32).rearrange("p t o -> p (t o)"), ALU.subtract).then_inc(w0_done, 1)
            dve.wait_ge(consts, 2)
            dve.wait_ge(small_in, 16 * 7)

            def split_weights(layer):
                for g in range(NG):
                    n = layer * NG + g
                    size = group_cols(g)
                    cols = slice(2 * g * O, 2 * g * O + size)
                    dve.wait_ge(w_hi_done, 2 * n + 1)
                    nc.vector.tensor_tensor(w_lo[:, cols], stage[:, n % 2, 0, 0:size], w_hi[:, cols].bitcast(f32),
                                            ALU.subtract).then_inc(w_done, 1)
                    dve.wait_ge(w_hi_done, 2 * n + 2)
                    nc.vector.scalar_tensor_tensor(
                        out=w_st[0:RS, :, cols], in0=stack_hi[0:RS, :, 0:size], scalar=minus_lo_rows[0:RS, :],
                        in1=stage[0:RS, n % 2, 1:3, 0:size], op0=ALU.mult, op1=ALU.add).then_inc(w_done, 1)

            def prod_lo(c):
                dve.wait_ge(prodT_hi_done, c + 1)
                nc.vector.tensor_tensor(prodT_lo[:], prodT_ps[0:R0, 0:T0, :], prodT_hi[:].bitcast(f32),
                                        ALU.subtract).then_inc(prodT_lo_done, 1)

            def z0_bias(c):
                dve.wait_ge(z0_done, c + 1)
                wait(dve, hs_hi, 2 * c)
                wait(dve, hs_lo, c)
                wait(dve, sums0, c)
                nc.vector.tensor_tensor(z0_sb[:], z0_ps[:, 0:O], bias[:, 0, :], ALU.add).then_inc(z0_biased, 1)

            def hidden_lo(z, n):
                dve.wait_ge(hs_hi, 2 * n + 1)
                nc.vector.scalar_tensor_tensor(out=hs[:, O + GH:2 * O + GH], in0=z, scalar=0.0,
                                               in1=hs[:, 0:O].bitcast(f32), op0=ALU.max,
                                               op1=ALU.subtract).then_inc(hs_lo, 1)

            def add_to_sums(z, layer, c, s, count):
                to = top_x[:, c // D, layer * O:(layer + 1) * O]
                wait(dve, s, count)
                nc.vector.scalar_tensor_tensor(out=to, in0=z, scalar=0.0, in1=to, op0=ALU.max,
                                               op1=ALU.add).then_inc(s, 1)

            def prepare1(c, after):
                if after == 5:
                    prod_lo(c)
                if after == 12:
                    z0_bias(c)
                if after == 13:
                    dve.wait_ge(z0_biased, c + 1)
                    hidden_lo(z0_sb[:], c)
                    add_to_sums(z0_sb[:], 0, c, sums0, c)

            def take_x0(layer, c, u):
                n = (layer - 1) * NCH + c
                if layer == 1:
                    dve.wait_ge(prod_ready, c + 3)
                wait(dve, summed, F * (n - 1))
                nc.vector.tensor_scalar(x0[:, u, :], x0_all[:, c, 0:F], 1.0, None, ALU.mult).then_inc(x0_ready, 1)

            def layer_step(layer, c, u, last):
                n = (layer - 1) * NCH + c
                dve.wait_ge(x0_ready, n + 1)
                wait(dve, z_done, n - 1)
                for g in range(NG):
                    dve.wait_ge(y_done, NG * n + g + 1)
                    for f in range(2 * g, min(2 * g + 2, F)):
                        y = y_ps[:, g % NBANK, (f % 2) * O:(f % 2 + 1) * O]
                        scale = x0[:, u, f:f + 1]
                        to = acc[:, u, f % 2, :]
                        if f >= 2:
                            dve.wait_ge(summed, F * n + f - 1)
                        if f == 1:
                            nc.vector.tensor_scalar(to, y, scale, None, ALU.mult).then_inc(summed, 1)
                        else:
                            nc.vector.scalar_tensor_tensor(
                                out=to, in0=y, scalar=scale, in1=to if f else bias[:, layer, :],
                                op0=ALU.mult, op1=ALU.add).then_inc(summed, 1)
                    if not last:
                        if g == 15:
                            take_x0(layer, c + 1, 1 - u)
                        if layer == 1:
                            prepare1(c + 1, g)
                        elif g == 4:
                            dve.wait_ge(z1_loaded[1 - u], z1_count(c + 1, 1 - u))
                            hidden_lo(z1_in[:, 1 - u, :], NCH + c + 1)
                z = (z1_out if layer == 1 else z2_sb)[:, u, :]
                dve.wait_ge(summed, F * (n + 1))
                if layer == 1:
                    wait(dve, z1_stored[u], z1_count(c, u) - 16)
                wait(dve, sums12, n - 1)
                nc.vector.tensor_tensor(z, acc[:, u, 0, :], acc[:, u, 1, :], ALU.add).then_inc(z_done, 1)
                dve.wait_ge(z_done, n + 1)
                add_to_sums(z, layer, c, sums12, n)

            def z1_count(c, u):
                return 8 * (c - u) + 16

            split_weights(0)
            for g in range(NG):
                prepare1(0, g)
            take_x0(1, 0, 0)
            over_chunks(dve, lambda c, u, last: layer_step(1, c, u, last))
            dve.wait_ge(z1_loaded[0], 16)
            split_weights(1)
            take_x0(2, 0, 0)
            hidden_lo(z1_in[:, 0, :], NCH)
            over_chunks(dve, lambda c, u, last: layer_step(2, c, u, last))

            dve.wait_ge(xT_ps_done, 2)
            nc.vector.tensor_copy(xT[:, 2:4, :], y_ps[:, 2:4, :]).then_inc(xT_done, 1)
            tail = TOP_IN - (KT1 - 1) * P
            nc.vector.tensor_copy(xT[0:tail, KT1 - 1, :], prodT_ps[0:tail, 0:4, :].rearrange("p a n -> p (a n)")).then_inc(xT_done, 1)

        @block.tensor
        def _(pe):
            pe.wait_ge(consts, 1)

            def transpose(to, src):
                return nc.tensor.transpose(to, src, ident[:])

            def prod_T(c, u):
                if isinstance(c, int) and c < 2:
                    pe.wait_ge(prod_ready, 2 + c + 1)
                else:
                    pe.wait_ge(prod_ready, c + 3)
                wait(pe, prodT_lo_done, c)
                for t in range(T0):
                    last = transpose(prodT_ps[0:R0, t, :], prod[:, u, t * R0:(t + 1) * R0])
                last.then_inc(prodT_done, 1)

            def layer0(c):
                pe.wait_ge(prodT_lo_done, c + 1)
                pe.wait_ge(w0_done, 1)
                wait(pe, z0_biased, c)
                for t in range(T0):
                    for a, w in ((prodT_hi, w0_hi), (prodT_lo, w0_hi), (prodT_hi, w0_lo)):
                        last = nc.tensor.matmul(z0_ps[:, 0:O], a[:, t, :], w[:, t, :], start=t == 0 and a is prodT_hi and w is w0_hi,
                                                stop=t == T0 - 1 and w is w0_lo)
                last.then_inc(z0_done, 1)

            def hidden_T(n):
                pe.wait_ge(hs_hi, 2 * n + 2)
                pe.wait_ge(hs_lo, n + 1)
                wait(pe, hT_ready, 2 * n)
                src = hs[:].bitcast(f32)
                low = GA + RS
                transpose(hT_ps[:, 0, :], src[:, 0:GA])
                transpose(hT_ps[:, 1, :], src[:, low:low + GA])
                transpose(hT_ps[0:RS, 2, :], src[:, GA:low])
                transpose(hT_ps[0:RS, 3, :], src[:, low + GA:low + low]).then_inc(hT_done, 1)

            def prepare1(c, u, before):
                if before == 2:
                    prod_T(c, u)
                if before == 9:
                    layer0(c)
                if before == 17:
                    hidden_T(c)

            def layer_step(layer, c, u, last):
                n = (layer - 1) * NCH + c
                pe.wait_ge(hT_ready, 2 * n + 2)
                for g in range(NG):
                    if not last:
                        if layer == 1:
                            prepare1(c + 1, 1 - u, g)
                        elif g == 12:
                            hidden_T(n + 1)
                    if isinstance(c, int) and c == 0:
                        pe.wait_ge(w_done, 2 * ((layer - 1) * NG + g + 1))
                    wait(pe, summed, bank_free(n, g))
                    size = group_cols(g)
                    cols = slice(2 * g * O, 2 * g * O + size)
                    y = y_ps[:, g % NBANK, 0:size]
                    nc.tensor.matmul(y, hT[:, u, 0, :], w_hi[:, cols], start=True, stop=False)
                    nc.tensor.matmul(y, hT[:, u, 1, :], w_hi[:, cols], start=False, stop=False)
                    nc.tensor.matmul(y, hT[:, u, 0, :], w_lo[:, cols], start=False, stop=False)
                    nc.tensor.matmul(y, hT[0:RS, u, 2, :], w_st[0:RS, 0, cols], start=False, stop=False)
                    nc.tensor.matmul(y, hT[0:RS, u, 3, :], w_st[0:RS, 1, cols], start=False, stop=True).then_inc(y_done, 1)

            for g in range(NG):
                prepare1(0, 0, g)
            over_chunks(pe, lambda c, u, last: layer_step(1, c, u, last))
            hidden_T(NCH)
            over_chunks(pe, lambda c, u, last: layer_step(2, c, u, last))

            pe.wait_ge(sums12, 2 * NCH)
            for t in range(KT1):
                rows = min(P, TOP_IN - t * P)
                for b in range(NBLK):
                    to = y_ps[:, t, b * P:(b + 1) * P] if t < NBANK else prodT_ps[0:rows, b, :]
                    last = transpose(to, top_x[:, b, t * P:t * P + rows])
                if t in (1, KT1 - 1):
                    last.then_inc(xT_ps_done, 1)
            pe.wait_ge(xT_done, 3)
            pe.wait_ge(top_in, 16 * 3)
            for m in range(4):
                for t in range(KT1):
                    rows = min(P, TOP_IN - t * P)
                    last = nc.tensor.matmul(y_ps[:, m, :], wt1_sb[0:rows, t, m * P:(m + 1) * P], xT[0:rows, t, :],
                                            start=t == 0, stop=t == KT1 - 1)
                last.then_inc(top_mm, 1)
            pe.wait_ge(top_act, 4)
            two = prodT_ps[:].rearrange("p (t a) n -> p t (a n)", t=2)
            for m in range(2):
                for t in range(4):
                    last = nc.tensor.matmul(two[:, m, :], wt2_sb[:, t, m * P:(m + 1) * P], h1T[:, t, :],
                                            start=t == 0, stop=t == 3)
                last.then_inc(top_mm, 1)
            pe.wait_ge(top_act, 6)
            for t in range(2):
                last = nc.tensor.matmul(z0_ps[0:1, 0:B], wt3_sb[:, t:t + 1], h2T[:, t, :], start=t == 0, stop=t == 1)
            last.then_inc(top_mm, 1)


def kernel(**inputs):
    import numpy as np
    import concourse.bacc as bacc
    from concourse import mybir as mb
    from concourse.bass_utils import run_bass_kernel_spmd as run

    nc = bacc.Bacc("TRN2", target_bir_lowering=False, num_devices=1)
    arrays = {}

    def given(name, a):
        a = np.ascontiguousarray(a)
        arrays[name] = a
        return nc.dram_tensor(name, a.shape, mb.dt.from_np(a.dtype), kind="ExternalInput").ap()

    ids = given("ids_dram", inputs["ids"])
    tables = [given(f"tbl_{f}_dram", inputs[f"tbl_{f}"]) for f in range(F)]
    dense = given("dense_dram", inputs["dense_ctx"])
    f = np.tile(np.arange(F), K2)
    g = (f + np.repeat(np.arange(K2), F)) % F
    w0 = np.asarray(inputs["L0_rec_W0"])
    w0_a = given("w0_a_dram", w0[:, f, g].T)
    w0_b = given("w0_b_dram", w0[:, g[F:], f[F:]].T)
    w1, w2 = (given(f"w{n}_dram", np.asarray(inputs[f"L0_rec_W{n}"]).transpose(2, 1, 0).reshape(O, F * O)) for n in (1, 2))
    b = [given(f"b{n}_dram", inputs[f"L0_rec_b{n}"]) for n in range(3)]
    wt1 = given("wt1_dram", inputs["W_top1"])
    bt1 = given("bt1_dram", np.asarray(inputs["b_top1"]).reshape(4, P).T)
    wt2 = given("wt2_dram", inputs["W_top2"])
    bt2 = given("bt2_dram", np.asarray(inputs["b_top2"]).reshape(2, P).T)
    wt3 = given("wt3_dram", np.asarray(inputs["W_top3"]).reshape(2, P).T)
    out = nc.dram_tensor("y_dram", (B, 1), mb.dt.float32, kind="ExternalOutput").ap()
    dlrm_tower(nc, ids, tables, dense, w0_a, w0_b, w1, w2, *b, wt1, bt1, wt2, bt2, wt3, out)
    return run(nc, [arrays], core_ids=[0]).results[0]["y_dram"]
```

```python
import concourse.bass as bass
from concourse import mybir
from contextlib import ExitStack

P = 128
B = 512
F = 39
D = 16
O = 200
NBLK = B // P
NCH = NBLK * D
K2 = F // 2 + 1
FE = F + K2 - 1
KT = 3
T0 = -(-K2 // KT)
R0 = KT * F
NPAIR = K2 * F
GA = 128
GB = O - GA
GH = GB // 2
RS = GB + GH
NG = (F + 1) // 2
NBANK = 4
SCOL = 2 * (GA + RS)
TOP_IN = 3 * O + 16
M1, M2 = 512, 256
KT1 = -(-TOP_IN // P)


NSLOT = 4


def group_cols(g):
    return min(2, F - 2 * g) * O


def skewed(lead):
    return ([(0, g) for g in range(lead)] +
            [x for g in range(lead, NG) for x in ((0, g), (1, g - lead))] +
            [(1, g) for g in range(NG - lead, NG)])


CLOSING = skewed(9)
OPENING = skewed(5)


def stacks_by(engine, layer, g):
    mine = [n for n in range(layer * NG + g + 1) if (n >= NG and n % 2 == 1) == (engine == "pool")]
    return len(mine)


def dlrm_tower(nc, ids, tables, dense, w0_a, w0_b, w1, w2, b0, b1, b2, wt1, bt1, wt2, bt2, wt3, out):
    f32, f32r, i32 = mybir.dt.float32, mybir.dt.float32r, mybir.dt.int32
    ALU, ACT = mybir.AluOpType, mybir.ActivationFunctionType
    z1_dram = nc.dram_tensor("z1_between_phases", (NCH, P, O), f32, kind="Internal").ap()

    ctx = ExitStack()
    with ctx:
        def sb(name, shape, dt=f32):
            return ctx.enter_context(nc.sbuf_tensor(name, shape, dt))

        def pb(name, shape):
            return ctx.enter_context(nc.psum_tensor(name, shape, f32))

        def sem(name):
            return ctx.enter_context(nc.semaphore(name))

        w_hi = sb("w_hi", [GA, F * O], f32r)
        w_lo = sb("w_lo", [GA, F * O], f32r)
        w_st = sb("w_st", [P, 2, F * O], f32r)
        n_prod, n_stage, n_gath, n_x0 = 2 * T0 * R0, 2 * 3 * 2 * O, 2 * F * D, NCH * FE
        area = sb("area", [P, n_prod + n_stage + n_gath + n_x0])
        at_gath, at_stage = n_prod, n_prod + n_gath
        at_x0 = at_stage + n_stage
        prod = area[:, 0:n_prod].rearrange("p (u n) -> p u n", u=2)
        gath = area[:, at_gath:at_stage].rearrange("p (u f d) -> p u f d", u=2, d=D)
        x0_all = area[:, at_x0:at_x0 + n_x0].rearrange("p (c f) -> p c f", f=FE)

        def stage(layer, g):
            slot, size = g % NSLOT, 3 * 2 * O
            first = (at_stage + slot * size if slot < 2 else
                     (0 if layer else at_x0 + D * FE) + (slot - 2) * size)
            return area[:, first:first + size].rearrange("p (s n) -> p s n", s=3)

        at_top = KT1 * M1 + 4 * M2
        assert at_top <= at_x0 and at_top + (KT1 + 4) * B <= at_x0 + n_x0
        wt1_sb = area[:, 0:KT1 * M1].rearrange("p (t n) -> p t n", n=M1)
        wt2_sb = area[:, KT1 * M1:at_top].rearrange("p (t n) -> p t n", n=M2)
        xT = area[:, at_top:at_top + KT1 * B].rearrange("p (t n) -> p t n", n=B)
        h1T = area[:, at_top + KT1 * B:at_top + (KT1 + 4) * B].rearrange("p (t n) -> p t n", n=B)
        h2T = area[:, at_top:at_top + 2 * B].rearrange("p (t n) -> p t n", n=B)
        y_sb = area[0:1, at_top + 2 * B:at_top + 3 * B]

        w0 = sb("w0", [R0, T0, 2, O], f32r)
        prodT_hi = sb("prodT_hi", [R0, T0, P], f32r)
        prodT_lo = sb("prodT_lo", [R0, T0, P], f32r)
        top_x = sb("top_x", [P, NBLK, TOP_IN])
        hs = sb("hs", [P, SCOL], f32r)
        hT = sb("hT", [P, 2, 4, P], f32r)
        z0_sb = sb("z0_sb", [P, O])
        z1_out = sb("z1_out", [P, 2, O])
        z1_in = sb("z1_in", [P, 2, O])
        z2_sb = sb("z2_sb", [P, 2, O])
        acc = sb("acc", [P, 2, 2, O])
        x0 = sb("x0", [P, 2, F])
        bias = sb("bias", [P, 3, O])
        ids_sb = sb("ids_sb", [P, NBLK, F], i32)
        ident = sb("ident", [P, P])
        is_lo_row = sb("is_lo_row", [P, 1])
        bt1_sb = sb("bt1_sb", [P, 4])
        bt2_sb = sb("bt2_sb", [P, 2])
        wt3_sb = sb("wt3_sb", [P, 2])

        y_ps = pb("y_ps", [P, NBANK, 512])
        prodT_ps = pb("prodT_ps", [P, 8, P])
        z0_ps = pb("z0_ps", [P, 512])
        hT_ps = pb("hT_ps", [P, 4, P])

        ids_in = sem("ids_in")
        w0_in = sem("w0_in")
        bias_in = sem("bias_in")
        top_in = sem("top_in")
        raw_in = [sem(f"raw_in{u}") for u in range(NSLOT)]
        z1_loaded = [sem(f"z1_loaded{u}") for u in range(2)]
        z1_stored = [sem(f"z1_stored{u}") for u in range(2)]
        gathered = [sem(f"gathered{b}") for b in range(NBLK)]
        out_stored = sem("out_stored")
        blank = sem("blank")
        w0_blank = sem("w0_blank")
        consts = sem("consts")
        w0_sum = sem("w0_sum")
        w0_hi_done = sem("w0_hi_done")
        w0_done = sem("w0_done")
        top_blank = sem("top_blank")
        w_hi_done = sem("w_hi_done")
        w_lo_done = sem("w_lo_done")
        w_st_dve = sem("w_st_dve")
        w_st_pool = sem("w_st_pool")
        pads = sem("pads")
        x0_first = sem("x0_first")
        x0_block = sem("x0_block")
        x0_ready = sem("x0_ready")
        first_prod = sem("first_prod")
        prod_ready = sem("prod_ready")
        prodT_done = sem("prodT_done")
        prodT_hi_done = sem("prodT_hi_done")
        prodT_lo_done = sem("prodT_lo_done")
        z0_done = sem("z0_done")
        z0_part = sem("z0_part")
        z0_biased = sem("z0_biased")
        hs_hi = sem("hs_hi")
        hs_lo = sem("hs_lo")
        hT_done = sem("hT_done")
        hT_ready = sem("hT_ready")
        y_done = sem("y_done")
        summed = sem("summed")
        z_done = sem("z_done")
        sums0 = sem("sums0")
        sums12 = sem("sums12")
        xT_ps_done = sem("xT_ps_done")
        xT_done = sem("xT_done")
        top_mm = sem("top_mm")
        top_act = sem("top_act")

        block = ctx.enter_context(nc.Block())

        def wait(eng, s, count):
            if not isinstance(count, int) or count > 0:
                eng.wait_ge(s, count)

        def over_middle(eng, step):
            with eng.Fori(1, NCH // 2 - 1) as i:
                step(2 * i, 0)
                step(2 * i + 1, 1)

        def fields_in(order, count):
            return sum(min(2, F - 2 * g) for _, g in order[:count])

        ALONE = [(0, g) for g in range(NG)]

        def bank_free(n, order, pos):
            if pos >= NBANK:
                return n * F + fields_in(order, pos - NBANK + 1)
            return n * F - (F - fields_in(ALONE, pos - NBANK + 1 + NG))

        def top1_ps(m):
            return (prodT_ps[:, 4 * m:4 * m + 4, :].rearrange("p a n -> p (a n)") if m < 2 else
                    z0_ps[:, 0:B] if m == 2 else hT_ps[:].rearrange("p a n -> p (a n)"))

        def top_xT_ps(t):
            return top1_ps(t) if t < 3 else y_ps[:, t - 3, :]

        def hT_free(n):
            if isinstance(n, int) and n == NCH:
                return NG * (NCH - 2) + CLOSING.index((0, NG - 1)) + 1
            if isinstance(n, int) and n == NCH + 2:
                return NG * NCH + OPENING.index((0, NG - 1)) + 1
            return NG * (n - 1)

        def w_released(g):
            return NG * (NCH - 2) + CLOSING.index((1, g)) + 1

        def wait_split(eng, layer, g):
            eng.wait_ge(w_lo_done, layer * NG + g + 1)
            eng.wait_ge(w_st_dve, stacks_by("dve", layer, g))
            wait(eng, w_st_pool, stacks_by("pool", layer, g))

        def chunk_major(engine, b, d0, d1, s):
            to = x0_all[:, b * D + d0:b * D + d1, :]
            rows = gath[:, b % 2, :, d0:d1].rearrange("p f d -> p d f")
            engine.tensor_copy(to[:, :, 0:F], rows).then_inc(s, 1)
            engine.tensor_copy(to[:, :, F:FE], rows[:, :, 0:FE - F]).then_inc(s, 1)

        def products(engine, c, u):
            row = x0_all[:, c, :]
            near = row[:, 0:F].unsqueeze(1).to_broadcast([P, K2, F])
            far = bass.AP(tensor=row.tensor, offset=row.offset, ap=[list(row.ap[0]), [1, K2], [1, F]])
            return engine.tensor_tensor(prod[:, u, 0:NPAIR].rearrange("p (k f) -> p k f", f=F), near, far, ALU.mult)

        def split_lo(engine, layer, g):
            size = group_cols(g)
            cols = slice(2 * g * O, 2 * g * O + size)
            return engine.tensor_tensor(w_lo[:, cols], stage(layer, g)[:, 0, 0:size], w_hi[:, cols].bitcast(f32),
                                        ALU.subtract)

        def split_stack(engine, layer, g):
            size = group_cols(g)
            to = w_st[0:RS, :, 2 * g * O:2 * g * O + size]
            return engine.tensor_tensor(to, stage(layer, g)[0:RS, 1:3, 0:size], to.bitcast(f32), ALU.subtract)

        @block.sync
        def _(sp):
            sp.dma_start(ids_sb[:], ids.rearrange("(b p) f -> p b f", p=P)).then_inc(ids_in, 16)
            a_raw = area[:, 0:T0 * O].rearrange("p (t o) -> p t o", o=O)
            b_raw = top_x[:].rearrange("p b n -> p (b n)")[:, 0:T0 * O].rearrange("p (t o) -> p t o", o=O)
            full = (T0 - 1) * R0
            last = NPAIR - full
            sp.wait_ge(w0_blank, 3)
            sp.dma_start(a_raw[0:R0, 0:T0 - 1, :], w0_a[0:full, :].rearrange("(t p) o -> p t o", p=R0)).then_inc(w0_in, 16)
            sp.dma_start(a_raw[0:last, T0 - 1, :], w0_a[full:NPAIR, :]).then_inc(w0_in, 16)
            sp.dma_start(b_raw[F:R0, 0, :], w0_b[0:R0 - F, :]).then_inc(w0_in, 16)
            sp.dma_start(b_raw[0:R0, 1:T0 - 1, :], w0_b[R0 - F:full - F, :].rearrange("(t p) o -> p t o", p=R0)).then_inc(w0_in, 16)
            sp.dma_start(b_raw[0:last, T0 - 1, :], w0_b[full - F:NPAIR - F, :]).then_inc(w0_in, 16)

            def load_group(w, layer, g):
                n = layer * NG + g
                size = group_cols(g)
                cols = slice(2 * g * O, 2 * g * O + size)
                to = stage(layer, g)[:, :, 0:size]
                low = w[GA:O, cols]
                if g >= NSLOT:
                    wait_split(sp, layer, g - NSLOT)
                elif layer:
                    wait_split(sp, 0, NG - 1)
                sp.dma_start(to[:, 0, :], w[0:GA, cols]).then_inc(raw_in[n % NSLOT], 16)
                sp.dma_start(to[0:GB, 1:3, :], low.unsqueeze(1).to_broadcast([GB, 2, size])).then_inc(raw_in[n % NSLOT], 16)
                sp.dma_start(to[GB:RS, 1:3, :], low.rearrange("(s p) n -> p s n", s=2)).then_inc(raw_in[n % NSLOT], 16)

            for g in range(NG):
                load_group(w1, 0, g)
                if g == 10:
                    for l, b in enumerate((b0, b1, b2)):
                        sp.dma_start(bias[:, l, :], b.rearrange("(a n) -> a n", a=1).to_broadcast([P, O])).then_inc(bias_in, 16)
            sp.wait_ge(top_blank, 1)
            sp.dma_start(top_x[:, :, 3 * O:TOP_IN], dense.rearrange("(b p) n -> p b n", p=P)).then_inc(top_in, 16)
            sp.dma_start(bt1_sb[:], bt1).then_inc(top_in, 16)
            sp.dma_start(bt2_sb[:], bt2).then_inc(top_in, 16)
            sp.dma_start(wt3_sb[:], wt3).then_inc(top_in, 16)

            def load_z1(c, u):
                wait(sp, hs_hi, 2 * (NCH + c - 1))
                wait(sp, hs_lo, NCH + c - 1)
                sp.dma_start(z1_in[:, u, :], z1_dram[c, :, :]).then_inc(z1_loaded[u], 16)

            def store_z1(c, u):
                sp.wait_ge(z_done, c + 1)
                sp.dma_start(z1_dram[c, :, :], z1_out[:, u, :]).then_inc(z1_stored[u], 16)

            store_z1(0, 0)
            store_z1(1, 1)
            over_middle(sp, store_z1)
            for u in range(2):
                sp.wait_ge(z1_stored[u], 16 * (NCH // 2 - 1))
                sp.dma_start(z1_in[:, u, :], z1_dram[u, :, :]).then_inc(z1_loaded[u], 16)
            for g in range(NG):
                if g == 2:
                    sp.wait_ge(prodT_done, NCH)
                load_group(w2, 1, g)
            store_z1(NCH - 2, 0)
            store_z1(NCH - 1, 1)
            load_z1(2, 0)
            load_z1(3, 1)
            wait_split(sp, 1, NG - 1)
            full = (KT1 - 1) * P
            sp.dma_start(wt1_sb[:, 0:KT1 - 1, :], wt1[0:full, :].rearrange("(t p) n -> p t n", p=P)).then_inc(top_in, 16)
            sp.dma_start(wt1_sb[0:TOP_IN - full, KT1 - 1, :], wt1[full:TOP_IN, :]).then_inc(top_in, 16)
            sp.dma_start(wt2_sb, wt2.rearrange("(t p) n -> p t n", p=P)).then_inc(top_in, 16)
            for u in range(2):
                sp.wait_ge(z1_stored[u], 16 * NCH // 2)
            with sp.Fori(2, NCH // 2) as i:
                load_z1(2 * i, 0)
                load_z1(2 * i + 1, 1)
            sp.wait_ge(top_act, 7)
            sp.dma_start(out.rearrange("b a -> a b"), y_sb).then_inc(out_stored, 16)
            sp.wait_ge(out_stored, 16)

        @block.gpsimd
        def _(pool):
            nc.gpsimd.memset(ident[:], 0.0).then_inc(blank, 1)
            nc.gpsimd.memset(is_lo_row[:], 0.0).then_inc(blank, 1)
            pool.wait_ge(blank, 2)
            nc.gpsimd.affine_select(out=ident[:], in_=ident[:], compare_op=ALU.not_equal, fill=1.0, base=0,
                                    pattern=[[-1, P]], channel_multiplier=1).then_inc(consts, 1)
            nc.gpsimd.affine_select(out=is_lo_row[:], in_=is_lo_row[:], compare_op=ALU.is_ge, fill=1.0,
                                    base=GB - 1, pattern=[[0, 1]], channel_multiplier=-1).then_inc(consts, 1)

            def gather(b, f):
                nc.gpsimd.indirect_dma_start(
                    gath[:, b % 2, f, :], None, tables[f],
                    bass.IndirectOffsetOnAxis(ap=ids_sb[:, b, f:f + 1], axis=0)).then_inc(gathered[b], 16)

            def next_products(c, u, blocks):
                wait(pool, prodT_done, c - 1)
                pool.wait_ge(x0_block, 2 * blocks)
                products(nc.gpsimd, c, u).then_inc(prod_ready, 1)

            pool.wait_ge(ids_in, 16)
            for f in range(F):
                gather(0, f)
            pool.wait_ge(pads, 2)
            per_chunk = -(-F // (D - 3))
            for b in range(NBLK - 1):
                for d in range(D):
                    if b or d:
                        next_products(b * D + d, d % 2, b + 1)
                    for f in range(per_chunk * d, min(per_chunk * (d + 1), F)):
                        gather(b + 1, f)
                pool.wait_ge(gathered[b + 1], 16 * F)
                if b == 0:
                    wait_split(pool, 0, NG - 1)
                chunk_major(nc.gpsimd, b + 1, 0, D, x0_block)
            with pool.Fori(0, D // 2) as i:
                for u in range(2):
                    next_products((NBLK - 1) * D + 2 * i + u, u, NBLK)

            for g in range(NG):
                pool.wait_ge(w_hi_done, 2 * (NG + g) + 1)
                split_lo(nc.gpsimd, 1, g).then_inc(w_lo_done, 1)
                if stacks_by("pool", 1, g) > stacks_by("pool", 1, g - 1):
                    pool.wait_ge(w_hi_done, 2 * (NG + g) + 2)
                    split_stack(nc.gpsimd, 1, g).then_inc(w_st_pool, 1)

        @block.scalar
        def _(act):
            act.wait_ge(w0_sum, 1)
            nc.scalar.activation(w0[:, :, 0, :], area[0:R0, 0:T0 * O].rearrange("p (t o) -> p t o", o=O),
                                 ACT.Copy).then_inc(w0_hi_done, 1)

            def round_weights(layer, groups):
                for g in groups:
                    n = layer * NG + g
                    size = group_cols(g)
                    cols = slice(2 * g * O, 2 * g * O + size)
                    act.wait_ge(raw_in[n % NSLOT], 16 * 3 * (n // NSLOT + 1))
                    if layer:
                        act.wait_ge(y_done, w_released(g))
                    nc.scalar.activation(w_hi[:, cols], stage(layer, g)[:, 0, 0:size], ACT.Copy).then_inc(w_hi_done, 1)
                    nc.scalar.activation(w_st[0:RS, :, cols], stage(layer, g)[0:RS, 1:3, 0:size], ACT.Copy,
                                         scale=is_lo_row[0:RS, :]).then_inc(w_hi_done, 1)

            def hidden_hi(z, n):
                wait(act, hT_done, n)
                nc.scalar.activation(hs[:, 0:O], z, ACT.Relu).then_inc(hs_hi, 1)
                twice = hs[:].rearrange("p (a n) -> p a n", a=2)[:, :, O:O + GH]
                nc.scalar.activation(twice, z[:, GA:O].rearrange("p (a n) -> p a n", a=2), ACT.Relu).then_inc(hs_hi, 1)

            def hidden_T(n, u):
                act.wait_ge(hT_done, n + 1)
                wait(act, y_done, hT_free(n))
                nc.scalar.activation(hT[:, u, 0:2, :], hT_ps[:, 0:2, :], ACT.Copy).then_inc(hT_ready, 1)
                nc.scalar.activation(hT[0:RS, u, 2:4, :], hT_ps[0:RS, 2:4, :], ACT.Copy).then_inc(hT_ready, 1)

            def prepare1(c, u):
                act.wait_ge(prodT_done, c + 1)
                wait(act, z0_done, c)
                nc.scalar.activation(prodT_hi[:], prodT_ps[0:R0, 0:T0, :], ACT.Copy).then_inc(prodT_hi_done, 1)
                act.wait_ge(z0_biased, c + 1)
                hidden_hi(z0_sb[:], c)
                hidden_T(c, u)

            def hidden2_hi(c, u):
                act.wait_ge(z1_loaded[u], z1_count(c, u))
                hidden_hi(z1_in[:, u, :], NCH + c)

            def prepare2(c, u):
                hidden2_hi(c, u)
                hidden_T(NCH + c, u)

            def z1_count(c, u):
                return 8 * (c - u) + 16

            act.wait_ge(consts, 2)
            round_weights(0, range(NG))
            for c in range(3):
                prepare1(c, c % 2)
            over_middle(act, lambda c, u: prepare1(c + 1, 1 - u))
            prepare1(NCH - 1, 1)
            hidden2_hi(0, 0)
            round_weights(1, range(0, 6))
            hidden2_hi(1, 1)
            round_weights(1, range(6, 11))
            hidden_T(NCH, 0)
            round_weights(1, range(11, 15))
            hidden_T(NCH + 1, 1)
            round_weights(1, range(15, NG))
            prepare2(2, 0)
            over_middle(act, lambda c, u: prepare2(c + 1, 1 - u))
            prepare2(NCH - 1, 1)

            act.wait_ge(top_in, 16 * 7)
            for t in range(KT1):
                rows = min(P, TOP_IN - t * P)
                act.wait_ge(xT_ps_done, t + 1)
                nc.scalar.activation(xT[0:rows, t, :], top_xT_ps(t)[0:rows, :], ACT.Copy).then_inc(xT_done, 1)
            for m in range(4):
                act.wait_ge(top_mm, m + 1)
                nc.scalar.activation(h1T[:, m, :], top1_ps(m), ACT.Relu, bias=bt1_sb[:, m:m + 1]).then_inc(top_act, 1)
            for m in range(2):
                act.wait_ge(top_mm, 5 + m)
                nc.scalar.activation(h2T[:, m, :], y_ps[:, m, :], ACT.Relu, bias=bt2_sb[:, m:m + 1]).then_inc(top_act, 1)
            act.wait_ge(top_mm, 7)
            nc.scalar.activation(y_sb, y_ps[0:1, 2, 0:B], ACT.Copy).then_inc(top_act, 1)

        @block.vector
        def _(dve):
            b_all = top_x[:].rearrange("p b n -> p (b n)")
            nc.vector.memset(area[:, (T0 - 1) * O:T0 * O], 0.0).then_inc(w0_blank, 1)
            nc.vector.memset(b_all[:, (T0 - 1) * O:T0 * O], 0.0).then_inc(w0_blank, 1)
            nc.vector.memset(b_all[:, 0:O], 0.0).then_inc(w0_blank, 1)
            a_raw = area[0:R0, 0:T0 * O]
            b_raw = top_x[:].rearrange("p b n -> p (b n)")[0:R0, 0:T0 * O]
            dve.wait_ge(w0_in, 5 * 16)
            nc.vector.tensor_tensor(a_raw, a_raw, b_raw, ALU.add).then_inc(w0_sum, 1)
            dve.wait_ge(w0_sum, 1)
            nc.vector.memset(top_x[:], 0.0).then_inc(top_blank, 1)
            dve.wait_ge(w0_hi_done, 1)
            nc.vector.tensor_tensor(w0[:, :, 1, :], a_raw.rearrange("p (t o) -> p t o", o=O),
                                    w0[:, :, 0, :].bitcast(f32), ALU.subtract).then_inc(w0_done, 1)
            dve.wait_ge(w0_done, 1)
            for u in range(2):
                nc.vector.memset(prod[:, u, NPAIR:T0 * R0], 0.0).then_inc(pads, 1)

            def prod_lo(c):
                dve.wait_ge(prodT_hi_done, c + 1)
                nc.vector.tensor_tensor(prodT_lo[:], prodT_ps[0:R0, 0:T0, :], prodT_hi[:].bitcast(f32),
                                        ALU.subtract).then_inc(prodT_lo_done, 1)

            def z0_bias(c):
                dve.wait_ge(z0_done, c + 1)
                wait(dve, hs_hi, 2 * c)
                wait(dve, hs_lo, c)
                wait(dve, sums0, c)
                nc.vector.tensor_tensor(z0_sb[:], z0_ps[:, 0:O], bias[:, 0, :], ALU.add).then_inc(z0_part, 1)
                dve.wait_ge(z0_part, c + 1)
                nc.vector.tensor_tensor(z0_sb[:], z0_ps[:, O:2 * O], z0_sb[:], ALU.add).then_inc(z0_biased, 1)

            def hidden_lo(z, n):
                dve.wait_ge(hs_hi, 2 * n + 1)
                nc.vector.scalar_tensor_tensor(out=hs[:, O + GH:2 * O + GH], in0=z, scalar=0.0,
                                               in1=hs[:, 0:O].bitcast(f32), op0=ALU.max,
                                               op1=ALU.subtract).then_inc(hs_lo, 1)

            def add_to_sums(z, layer, c, s, count):
                to = top_x[:, c // D, layer * O:(layer + 1) * O]
                wait(dve, s, count)
                nc.vector.scalar_tensor_tensor(out=to, in0=z, scalar=0.0, in1=to, op0=ALU.max,
                                               op1=ALU.add).then_inc(s, 1)

            def hidden0_lo(c):
                dve.wait_ge(z0_biased, c + 1)
                hidden_lo(z0_sb[:], c)
                add_to_sums(z0_sb[:], 0, c, sums0, c)

            def hidden2_lo(c, u):
                dve.wait_ge(z1_loaded[u], z1_count(c, u))
                hidden_lo(z1_in[:, u, :], NCH + c)

            def take_x0(n, u):
                c = n % NCH if isinstance(n, int) else n
                if isinstance(n, int) and n < NCH:
                    dve.wait_ge(x0_block, 2 * (n // D + 1))
                wait(dve, z_done, n - 1)
                nc.vector.tensor_scalar(x0[:, u, :], x0_all[:, c, 0:F], 1.0, None, ALU.mult).then_inc(x0_ready, 1)

            def scale_group(layer, n, u, g, bank, y_count, done):
                dve.wait_ge(y_done, y_count)
                if g == 0:
                    dve.wait_ge(x0_ready, n + 1)
                    wait(dve, z_done, n - 1)
                for f in range(2 * g, min(2 * g + 2, F)):
                    y = y_ps[:, bank, (f % 2) * O:(f % 2 + 1) * O]
                    scale = x0[:, u, f:f + 1]
                    to = acc[:, u, f % 2, :]
                    if f == 1:
                        nc.vector.tensor_scalar(to, y, scale, None, ALU.mult).then_inc(summed, 1)
                    else:
                        if f:
                            dve.wait_ge(summed, done + f % 2)
                        nc.vector.scalar_tensor_tensor(
                            out=to, in0=y, scalar=scale, in1=to if f else bias[:, layer, :],
                            op0=ALU.mult, op1=ALU.add).then_inc(summed, 1)

            def finish_z(layer, n, u, done):
                c = n - (layer - 1) * NCH
                z = (z1_out if layer == 1 else z2_sb)[:, u, :]
                dve.wait_ge(summed, done)
                if layer == 1:
                    wait(dve, z1_stored[u], z1_count(c, u) - 16)
                wait(dve, sums12, n - 1)
                nc.vector.tensor_tensor(z, acc[:, u, 0, :], acc[:, u, 1, :], ALU.add).then_inc(z_done, 1)
                dve.wait_ge(z_done, n + 1)
                add_to_sums(z, layer, c, sums12, n)

            def z1_count(c, u):
                return 8 * (c - u) + 16

            def step1(c, u):
                for g in range(NG):
                    scale_group(1, c, u, g, g % NBANK, NG * c + g + 1, F * c + 2 * g - 1)
                    if g == 5:
                        prod_lo(c + 1)
                    if g == 12:
                        z0_bias(c + 1)
                    if g == 13:
                        hidden0_lo(c + 1)
                    if g == 15:
                        dve.wait_ge(prod_ready, c + 1)
                        take_x0(c + 1, 1 - u)
                finish_z(1, c, u, F * (c + 1))

            def step2(c, u, last=False):
                n = NCH + c
                for g in range(NG):
                    scale_group(2, n, u, g, g % NBANK, NG * n + g + 1, F * n + 2 * g - 1)
                    if g == 4 and not last:
                        hidden2_lo(c + 1, 1 - u)
                    if g == 15 and not last:
                        wait(dve, z_done, n)
                        nc.vector.tensor_scalar(x0[:, 1 - u, :], x0_all[:, c + 1, 0:F], 1.0, None,
                                                ALU.mult).then_inc(x0_ready, 1)
                finish_z(2, n, u, F * (n + 1))

            def split_due(g):
                return 15 + 2 * g

            def pair_step(layer, order, n, due_from, between):
                for pos, (u, g) in enumerate(order):
                    scale_group(layer, n + u, u, g, pos % NBANK, NG * n + pos + 1, accumulated(order, n, pos))
                    if g == NG - 1:
                        finish_z(layer, n + u, u, n * F + fields_in(order, pos + 1))
                    between(pos)
                    for g2 in range(NG):
                        if split_due(g2) == due_from + pos and (g2 == 0 or True) and \
                                stacks_by("dve", 1, g2) > stacks_by("dve", 1, g2 - 1):
                            dve.wait_ge(w_hi_done, 2 * (NG + g2) + 2)
                            split_stack(nc.vector, 1, g2).then_inc(w_st_dve, 1)

            def accumulated(order, n, pos):
                u, g = order[pos]
                if g == 0:
                    return 0
                return n * F + fields_in(order, order.index((u, g - 1))) + 1

            for g in range(NG):
                dve.wait_ge(w_hi_done, 2 * g + 1)
                split_lo(nc.vector, 0, g).then_inc(w_lo_done, 1)
                dve.wait_ge(w_hi_done, 2 * g + 2)
                split_stack(nc.vector, 0, g).then_inc(w_st_dve, 1)
            dve.wait_ge(gathered[0], 16 * F)
            chunk_major(nc.vector, 0, 0, 1, x0_first)
            dve.wait_ge(x0_first, 2)
            products(nc.vector, 0, 0).then_inc(first_prod, 1)
            chunk_major(nc.vector, 0, 1, D, x0_block)
            dve.wait_ge(bias_in, 16 * 3)
            prod_lo(0)
            take_x0(0, 0)
            z0_bias(0)
            hidden0_lo(0)
            step1(0, 0)
            step1(1, 1)
            over_middle(dve, step1)

            def between_closing(pos):
                if pos == 1:
                    prod_lo(NCH - 1)
                if pos == 3:
                    z0_bias(NCH - 1)
                if pos == 4:
                    hidden0_lo(NCH - 1)
                if pos == 5:
                    take_x0(NCH - 1, 1)
                if pos == 14:
                    hidden2_lo(0, 0)
                if pos == 26:
                    hidden2_lo(1, 1)
                if pos == 33:
                    take_x0(NCH, 0)

            def between_opening(pos):
                if pos == 1:
                    take_x0(NCH + 1, 1)
                if pos == 10:
                    hidden2_lo(2, 0)
                if pos == 36:
                    take_x0(NCH + 2, 0)

            pair_step(1, CLOSING, NCH - 2, 0, between_closing)
            pair_step(2, OPENING, NCH, 2 * NG, between_opening)
            over_middle(dve, step2)
            step2(NCH - 2, 0)
            step2(NCH - 1, 1, last=True)

        @block.tensor
        def _(pe):
            pe.wait_ge(consts, 1)

            def transpose(to, src):
                return nc.tensor.transpose(to, src, ident[:])

            def prod_T(c, u):
                if isinstance(c, int) and c == 0:
                    pe.wait_ge(first_prod, 1)
                else:
                    pe.wait_ge(prod_ready, c)
                wait(pe, prodT_lo_done, c)
                for t in range(T0):
                    last = transpose(prodT_ps[0:R0, t, :], prod[:, u, t * R0:(t + 1) * R0])
                last.then_inc(prodT_done, 1)

            def layer0(c):
                pe.wait_ge(prodT_lo_done, c + 1)
                wait(pe, z0_biased, c)
                for t in range(T0):
                    hi = lambda: nc.tensor.matmul(z0_ps[:, 0:2 * O], prodT_hi[:, t, :], w0[:, t, :, :],
                                                  start=t == 0, stop=t == T0 - 1)
                    lo = lambda: nc.tensor.matmul(z0_ps[:, 0:O], prodT_lo[:, t, :], w0[:, t, 0, :], start=False, stop=False)
                    if t == 0:
                        hi()
                        lo()
                    else:
                        lo()
                        last = hi()
                last.then_inc(z0_done, 1)

            def hidden_T(n):
                pe.wait_ge(hs_hi, 2 * n + 2)
                pe.wait_ge(hs_lo, n + 1)
                wait(pe, hT_ready, 2 * n)
                src = hs[:].bitcast(f32)
                low = GA + RS
                transpose(hT_ps[:, 0, :], src[:, 0:GA])
                transpose(hT_ps[:, 1, :], src[:, low:low + GA])
                transpose(hT_ps[0:RS, 2, :], src[:, GA:low])
                transpose(hT_ps[0:RS, 3, :], src[:, low + GA:low + low]).then_inc(hT_done, 1)

            def group(n, u, g, bank, free):
                wait(pe, summed, free)
                size = group_cols(g)
                cols = slice(2 * g * O, 2 * g * O + size)
                y = y_ps[:, bank, 0:size]
                nc.tensor.matmul(y, hT[:, u, 0, :], w_hi[:, cols], start=True, stop=False)
                nc.tensor.matmul(y, hT[:, u, 1, :], w_hi[:, cols], start=False, stop=False)
                nc.tensor.matmul(y, hT[:, u, 0, :], w_lo[:, cols], start=False, stop=False)
                nc.tensor.matmul(y, hT[0:RS, u, 2, :], w_st[0:RS, 0, cols], start=False, stop=False)
                nc.tensor.matmul(y, hT[0:RS, u, 3, :], w_st[0:RS, 1, cols], start=False, stop=True).then_inc(y_done, 1)

            def step1(c, u):
                pe.wait_ge(hT_ready, 2 * c + 2)
                for g in range(NG):
                    if g == 2:
                        prod_T(c + 1, 1 - u)
                    if g == 9:
                        layer0(c + 1)
                    if g == 17:
                        hidden_T(c + 1)
                    if isinstance(c, int) and c == 0:
                        wait_split(pe, 0, g)
                    group(c, u, g, g % NBANK, bank_free(c, ALONE, g))

            def top_transpose(t):
                rows = min(P, TOP_IN - t * P)
                for b in range(NBLK):
                    last = transpose(top_xT_ps(t)[0:rows, b * P:(b + 1) * P], top_x[:, b, t * P:t * P + rows])
                last.then_inc(xT_ps_done, 1)

            def top_layer1(tiles):
                for t in tiles:
                    rows = min(P, TOP_IN - t * P)
                    pe.wait_ge(xT_done, t + 1)
                    for m in range(4):
                        last = nc.tensor.matmul(top1_ps(m), wt1_sb[0:rows, t, m * P:(m + 1) * P], xT[0:rows, t, :],
                                                start=t == 0, stop=t == KT1 - 1)
                        if t == KT1 - 1:
                            last.then_inc(top_mm, 1)

            def step2(c, u, last=False):
                n = NCH + c
                pe.wait_ge(hT_ready, 2 * n + 2)
                for g in range(NG):
                    if g == 12 and not last:
                        hidden_T(n + 1)
                    if last and g == 10:
                        pe.wait_ge(sums0, NCH)
                        pe.wait_ge(sums12, NCH)
                        for t in range(3):
                            top_transpose(t)
                    group(n, u, g, g % NBANK, bank_free(n, ALONE, g))

            prod_T(0, 0)
            pe.wait_ge(w0_done, 1)
            layer0(0)
            hidden_T(0)
            step1(0, 0)
            step1(1, 1)
            over_middle(pe, step1)
            for pos, (u, g) in enumerate(CLOSING):
                if pos == 0:
                    prod_T(NCH - 1, 1)
                if pos == 3:
                    layer0(NCH - 1)
                if pos == 7:
                    hidden_T(NCH - 1)
                if pos == 20:
                    hidden_T(NCH)
                if pos == 37:
                    hidden_T(NCH + 1)
                if g == 0:
                    pe.wait_ge(hT_ready, 2 * (NCH - 2 + u) + 2)
                group(NCH - 2 + u, u, g, pos % NBANK, bank_free(NCH - 2, CLOSING, pos))
            for pos, (u, g) in enumerate(OPENING):
                if pos == 20:
                    hidden_T(NCH + 2)
                if g == 0:
                    pe.wait_ge(hT_ready, 2 * (NCH + u) + 2)
                if u == 0:
                    wait_split(pe, 1, g)
                group(NCH + u, u, g, pos % NBANK, bank_free(NCH, OPENING, pos))
            over_middle(pe, step2)
            step2(NCH - 2, 0)
            step2(NCH - 1, 1, last=True)

            pe.wait_ge(top_in, 16 * 7)
            pe.wait_ge(xT_done, 3)
            top_layer1([0, 1])
            pe.wait_ge(sums12, 2 * NCH)
            top_transpose(3)
            top_transpose(4)
            top_layer1([2, 3, 4])
            for m in range(2):
                for t in range(4):
                    if m == 0:
                        pe.wait_ge(top_act, t + 1)
                    if t == 0:
                        pe.wait_ge(xT_done, KT1)
                    last = nc.tensor.matmul(y_ps[:, m, :], wt2_sb[:, t, m * P:(m + 1) * P], h1T[:, t, :],
                                            start=t == 0, stop=t == 3)
                last.then_inc(top_mm, 1)
            for t in range(2):
                pe.wait_ge(top_act, 5 + t)
                last = nc.tensor.matmul(y_ps[0:1, 2, 0:B], wt3_sb[:, t:t + 1], h2T[:, t, :], start=t == 0, stop=t == 1)
            last.then_inc(top_mm, 1)


def kernel(**inputs):
    import numpy as np
    import concourse.bacc as bacc
    from concourse import mybir as mb
    from concourse.bass_utils import run_bass_kernel_spmd as run

    nc = bacc.Bacc("TRN2", target_bir_lowering=False, num_devices=1)
    arrays = {}

    def given(name, a):
        a = np.ascontiguousarray(a)
        arrays[name] = a
        return nc.dram_tensor(name, a.shape, mb.dt.from_np(a.dtype), kind="ExternalInput").ap()

    ids = given("ids_dram", inputs["ids"])
    tables = [given(f"tbl_{f}_dram", inputs[f"tbl_{f}"]) for f in range(F)]
    dense = given("dense_dram", inputs["dense_ctx"])
    f = np.tile(np.arange(F), K2)
    g = (f + np.repeat(np.arange(K2), F)) % F
    w0 = np.asarray(inputs["L0_rec_W0"])
    w0_a = given("w0_a_dram", w0[:, f, g].T)
    w0_b = given("w0_b_dram", w0[:, g[F:], f[F:]].T)
    w1, w2 = (given(f"w{n}_dram", np.asarray(inputs[f"L0_rec_W{n}"]).transpose(2, 1, 0).reshape(O, F * O)) for n in (1, 2))
    b = [given(f"b{n}_dram", inputs[f"L0_rec_b{n}"]) for n in range(3)]
    wt1 = given("wt1_dram", inputs["W_top1"])
    bt1 = given("bt1_dram", np.asarray(inputs["b_top1"]).reshape(4, P).T)
    wt2 = given("wt2_dram", inputs["W_top2"])
    bt2 = given("bt2_dram", np.asarray(inputs["b_top2"]).reshape(2, P).T)
    wt3 = given("wt3_dram", np.asarray(inputs["W_top3"]).reshape(2, P).T)
    out = nc.dram_tensor("y_dram", (B, 1), mb.dt.float32, kind="ExternalOutput").ap()
    dlrm_tower(nc, ids, tables, dense, w0_a, w0_b, w1, w2, *b, wt1, bt1, wt2, bt2, wt3, out)
    return run(nc, [arrays], core_ids=[0]).results[0]["y_dram"]
```

```python
import concourse.bass as bass
from concourse import mybir
from contextlib import ExitStack

P = 128
B = 512
F = 39
D = 16
O = 200
NBLK = B // P
NCH = NBLK * D
K2 = F // 2 + 1
FE = F + K2 - 1
NPAIR = K2 * F
T0 = NPAIR // P
NREST = NPAIR - T0 * P
RREST = 3 * NREST
GA = 128
GB = O - GA
GH = GB // 2
RS = GB + GH
NG = (F + 1) // 2
NBANK = 4
BANK = 512
UNIT = 5
NU = -(-F // UNIT)
NY = 2 * NU
SCOL = 2 * (GA + RS)
TOP_IN = 3 * O + 16
M1, M2 = 512, 256
KT1 = -(-TOP_IN // P)


NSLOT = 4


def group_cols(g):
    return min(2, F - 2 * g) * O


def unit_fields(k):
    return range(UNIT * k, min(UNIT * (k + 1), F))


def half(k):
    return len(unit_fields(k)) * O // 2


def group_of(f):
    k = f // UNIT
    return 2 * k + ((f - UNIT * k + 1) * O > half(k))


def skewed(lead):
    return ([(0, k) for k in range(lead)] +
            [x for k in range(lead, NU) for x in ((0, k), (1, k - lead))] +
            [(1, k) for k in range(NU - lead, NU)])


ALONE = [(0, k) for k in range(NU)]
CLOSING = skewed(4)
OPENING = skewed(3)


def summed_after(order):
    fields = [(u, f) for u, k in order for f in unit_fields(k)]
    return {x: n + 1 for n, x in enumerate(fields)}


def groups_before(order, u, k):
    return 2 * order.index((u, k))


def stacks_by(engine, layer, g):
    mine = [n for n in range(layer * NG + g + 1) if (n >= NG and n % 2 == 1) == (engine == "pool")]
    return len(mine)


def dlrm_tower(nc, ids, tables, dense, w0_a, w0_b, w1, w2, b0, b1, b2, wt1, bt1, wt2, bt2, wt3, out):
    f32, f32r, i32 = mybir.dt.float32, mybir.dt.float32r, mybir.dt.int32
    ALU, ACT = mybir.AluOpType, mybir.ActivationFunctionType
    z1_dram = nc.dram_tensor("z1_between_phases", (NCH, P, O), f32, kind="Internal").ap()

    ctx = ExitStack()
    with ctx:
        def sb(name, shape, dt=f32):
            return ctx.enter_context(nc.sbuf_tensor(name, shape, dt))

        def pb(name, shape):
            return ctx.enter_context(nc.psum_tensor(name, shape, f32))

        def sem(name):
            return ctx.enter_context(nc.semaphore(name))

        w_hi = sb("w_hi", [GA, F * O], f32r)
        w_lo = sb("w_lo", [GA, F * O], f32r)
        w_st = sb("w_st", [P, 2, F * O], f32r)
        n_prod, n_stage, n_gath, n_x0 = 2 * NPAIR, 2 * 3 * 2 * O, 2 * F * D, NCH * FE
        area = sb("area", [P, n_prod + n_stage + n_gath + n_x0])
        at_gath, at_stage = n_prod, n_prod + n_gath
        at_x0 = at_stage + n_stage
        prod = area[:, 0:n_prod].rearrange("p (u n) -> p u n", u=2)
        gath = area[:, at_gath:at_stage].rearrange("p (u f d) -> p u f d", u=2, d=D)
        x0_all = area[:, at_x0:at_x0 + n_x0].rearrange("p (c f) -> p c f", f=FE)

        def stage(layer, g):
            slot, size = g % NSLOT, 3 * 2 * O
            first = (at_stage + slot * size if slot < 2 else
                     (0 if layer else at_x0 + D * FE) + (slot - 2) * size)
            return area[:, first:first + size].rearrange("p (s n) -> p s n", s=3)

        at_top = KT1 * M1 + 4 * M2
        assert at_top <= at_x0 and at_top + (KT1 + 4) * B <= at_x0 + n_x0
        wt1_sb = area[:, 0:KT1 * M1].rearrange("p (t n) -> p t n", n=M1)
        wt2_sb = area[:, KT1 * M1:at_top].rearrange("p (t n) -> p t n", n=M2)
        xT = area[:, at_top:at_top + KT1 * B].rearrange("p (t n) -> p t n", n=B)
        h1T = area[:, at_top + KT1 * B:at_top + (KT1 + 4) * B].rearrange("p (t n) -> p t n", n=B)
        h2T = area[:, at_top:at_top + 2 * B].rearrange("p (t n) -> p t n", n=B)
        y_sb = area[0:1, at_top + 2 * B:at_top + 3 * B]

        w0 = sb("w0", [P, T0, 2, O], f32r)
        w0_rest = sb("w0_rest", [RREST, O], f32r)
        rest = sb("rest", [P, RREST], f32r)
        restT = sb("restT", [RREST, P], f32r)
        prodT_hi = sb("prodT_hi", [P, T0, P], f32r)
        prodT_lo = sb("prodT_lo", [P, T0, P], f32r)
        top_x = sb("top_x", [P, NBLK, TOP_IN])
        hs = sb("hs", [P, SCOL], f32r)
        hT = sb("hT", [P, 2, 4, P], f32r)
        z0_sb = sb("z0_sb", [P, O])
        z1_out = sb("z1_out", [P, 2, O])
        z1_in = sb("z1_in", [P, 2, O])
        z2_sb = sb("z2_sb", [P, 2, O])
        acc = sb("acc", [P, 2, 2, O])
        x0 = sb("x0", [P, 2, F])
        bias = sb("bias", [P, 3, O])
        ids_sb = sb("ids_sb", [P, NBLK, F], i32)
        ident = sb("ident", [P, P])
        is_lo_row = sb("is_lo_row", [P, 1])
        is_rest_lo = sb("is_rest_lo", [P, 1])
        bt1_sb = sb("bt1_sb", [P, 4])
        bt2_sb = sb("bt2_sb", [P, 2])
        wt3_sb = sb("wt3_sb", [P, 2])

        y_ps = pb("y_ps", [P, NBANK, BANK])
        y_flat = y_ps[:].rearrange("p b n -> p (b n)")
        prodT_ps = pb("prodT_ps", [P, 8, P])
        z0_ps = pb("z0_ps", [P, 512])
        hT_ps = pb("hT_ps", [P, 4, P])

        ids_in = sem("ids_in")
        w0_in = sem("w0_in")
        bias_in = sem("bias_in")
        top_in = sem("top_in")
        raw_in = [sem(f"raw_in{u}") for u in range(NSLOT)]
        z1_loaded = [sem(f"z1_loaded{u}") for u in range(2)]
        z1_stored = [sem(f"z1_stored{u}") for u in range(2)]
        gathered = [sem(f"gathered{b}") for b in range(NBLK)]
        out_stored = sem("out_stored")
        blank = sem("blank")
        w0_blank = sem("w0_blank")
        consts = sem("consts")
        w0_sum = sem("w0_sum")
        w0_hi_done = sem("w0_hi_done")
        w0_done = sem("w0_done")
        top_blank = sem("top_blank")
        w_hi_done = sem("w_hi_done")
        w_lo_done = sem("w_lo_done")
        w_st_dve = sem("w_st_dve")
        w_st_pool = sem("w_st_pool")
        rest_hi = sem("rest_hi")
        rest_lo = sem("rest_lo")
        restT_done = sem("restT_done")
        x0_first = sem("x0_first")
        x0_block = sem("x0_block")
        x0_ready = sem("x0_ready")
        first_prod = sem("first_prod")
        prod_ready = sem("prod_ready")
        prodT_done = sem("prodT_done")
        prodT_hi_done = sem("prodT_hi_done")
        prodT_lo_done = sem("prodT_lo_done")
        z0_done = sem("z0_done")
        z0_part = sem("z0_part")
        z0_biased = sem("z0_biased")
        hs_hi = sem("hs_hi")
        hs_lo = sem("hs_lo")
        hT_done = sem("hT_done")
        hT_ready = sem("hT_ready")
        y_done = sem("y_done")
        summed = sem("summed")
        z_done = sem("z_done")
        sums0 = sem("sums0")
        sums12 = sem("sums12")
        xT_ps_done = sem("xT_ps_done")
        xT_done = sem("xT_done")
        top_mm = sem("top_mm")
        top_act = sem("top_act")

        block = ctx.enter_context(nc.Block())

        def wait(eng, s, count):
            if not isinstance(count, int) or count > 0:
                eng.wait_ge(s, count)

        def over_middle(eng, step):
            with eng.Fori(1, NCH // 2 - 1) as i:
                step(2 * i, 0)
                step(2 * i + 1, 1)

        def bank_free(n, order, pos):
            if pos < NBANK:
                n, order, pos = n - 1, ALONE, pos + NY
            u, k = order[(pos - NBANK) // 2]
            fields = unit_fields(k)
            last = max(f for f in fields if (f - fields[0]) * O < half(k)) if pos % 2 == 0 else fields[-1]
            return n * F + summed_after(order)[u, last]

        def top1_ps(m):
            return (prodT_ps[:, 4 * m:4 * m + 4, :].rearrange("p a n -> p (a n)") if m < 2 else
                    z0_ps[:, 0:B] if m == 2 else hT_ps[:].rearrange("p a n -> p (a n)"))

        def top_xT_ps(t):
            return top1_ps(t) if t < 3 else y_ps[:, t - 3, :]

        def hT_free(n):
            if isinstance(n, int) and n == NCH:
                return NY * (NCH - 2) + groups_before(CLOSING, 0, NU - 1) + 2
            if isinstance(n, int) and n == NCH + 2:
                return NY * NCH + groups_before(OPENING, 0, NU - 1) + 2
            return NY * (n - 1)

        def w_released(g):
            f = min(2 * g + 1, F - 1)
            return NY * (NCH - 2) + groups_before(CLOSING, 1, f // UNIT) + group_of(f) % 2 + 1

        def y_columns(bank, k):
            first = (bank + 1) * BANK - half(k)
            return y_flat[:, first:first + 2 * half(k)]

        def wait_split(eng, layer, g):
            eng.wait_ge(w_lo_done, layer * NG + g + 1)
            eng.wait_ge(w_st_dve, stacks_by("dve", layer, g))
            wait(eng, w_st_pool, stacks_by("pool", layer, g))

        def chunk_major(engine, b, d0, d1, s):
            to = x0_all[:, b * D + d0:b * D + d1, :]
            rows = gath[:, b % 2, :, d0:d1].rearrange("p f d -> p d f")
            engine.tensor_copy(to[:, :, 0:F], rows).then_inc(s, 1)
            engine.tensor_copy(to[:, :, F:FE], rows[:, :, 0:FE - F]).then_inc(s, 1)

        def products(engine, c, u):
            row = x0_all[:, c, :]
            near = row[:, 0:F].unsqueeze(1).to_broadcast([P, K2, F])
            far = bass.AP(tensor=row.tensor, offset=row.offset, ap=[list(row.ap[0]), [1, K2], [1, F]])
            return engine.tensor_tensor(prod[:, u, 0:NPAIR].rearrange("p (k f) -> p k f", f=F), near, far, ALU.mult)

        def split_lo(engine, layer, g):
            size = group_cols(g)
            cols = slice(2 * g * O, 2 * g * O + size)
            return engine.tensor_tensor(w_lo[:, cols], stage(layer, g)[:, 0, 0:size], w_hi[:, cols].bitcast(f32),
                                        ALU.subtract)

        def split_stack(engine, layer, g):
            size = group_cols(g)
            to = w_st[0:RS, :, 2 * g * O:2 * g * O + size]
            return engine.tensor_tensor(to, stage(layer, g)[0:RS, 1:3, 0:size], to.bitcast(f32), ALU.subtract)

        @block.sync
        def _(sp):
            sp.dma_start(ids_sb[:], ids.rearrange("(b p) f -> p b f", p=P)).then_inc(ids_in, 16)
            a_raw = area[:, 0:(T0 + 1) * O].rearrange("p (t o) -> p t o", o=O)
            b_raw = top_x[:].rearrange("p b n -> p (b n)")[:, 0:(T0 + 1) * O].rearrange("p (t o) -> p t o", o=O)
            full = T0 * P
            sp.wait_ge(w0_blank, 1)
            sp.dma_start(a_raw[:, 0:T0, :], w0_a[0:full, :].rearrange("(t p) o -> p t o", p=P)).then_inc(w0_in, 16)
            sp.dma_start(b_raw[F:P, 0, :], w0_b[0:P - F, :]).then_inc(w0_in, 16)
            sp.dma_start(b_raw[:, 1:T0, :], w0_b[P - F:full - F, :].rearrange("(t p) o -> p t o", p=P)).then_inc(w0_in, 16)
            for n in range(3):
                rows = slice(n * NREST, (n + 1) * NREST)
                sp.dma_start(a_raw[rows, T0, :], w0_a[full:NPAIR, :]).then_inc(w0_in, 16)
                sp.dma_start(b_raw[rows, T0, :], w0_b[full - F:NPAIR - F, :]).then_inc(w0_in, 16)

            def load_group(w, layer, g):
                n = layer * NG + g
                size = group_cols(g)
                cols = slice(2 * g * O, 2 * g * O + size)
                to = stage(layer, g)[:, :, 0:size]
                low = w[GA:O, cols]
                if g >= NSLOT:
                    wait_split(sp, layer, g - NSLOT)
                elif layer:
                    wait_split(sp, 0, NG - 1)
                sp.dma_start(to[:, 0, :], w[0:GA, cols]).then_inc(raw_in[n % NSLOT], 16)
                sp.dma_start(to[0:GB, 1:3, :], low.unsqueeze(1).to_broadcast([GB, 2, size])).then_inc(raw_in[n % NSLOT], 16)
                sp.dma_start(to[GB:RS, 1:3, :], low.rearrange("(s p) n -> p s n", s=2)).then_inc(raw_in[n % NSLOT], 16)

            for g in range(NG):
                load_group(w1, 0, g)
                if g == 10:
                    for l, b in enumerate((b0, b1, b2)):
                        sp.dma_start(bias[:, l, :], b.rearrange("(a n) -> a n", a=1).to_broadcast([P, O])).then_inc(bias_in, 16)
            sp.wait_ge(top_blank, 1)
            sp.dma_start(top_x[:, :, 3 * O:TOP_IN], dense.rearrange("(b p) n -> p b n", p=P)).then_inc(top_in, 16)
            sp.dma_start(bt1_sb[:], bt1).then_inc(top_in, 16)
            sp.dma_start(bt2_sb[:], bt2).then_inc(top_in, 16)
            sp.dma_start(wt3_sb[:], wt3).then_inc(top_in, 16)

            def load_z1(c, u):
                wait(sp, hs_hi, 2 * (NCH + c - 1))
                wait(sp, hs_lo, NCH + c - 1)
                sp.dma_start(z1_in[:, u, :], z1_dram[c, :, :]).then_inc(z1_loaded[u], 16)

            def store_z1(c, u):
                sp.wait_ge(z_done, c + 1)
                sp.dma_start(z1_dram[c, :, :], z1_out[:, u, :]).then_inc(z1_stored[u], 16)

            store_z1(0, 0)
            store_z1(1, 1)
            over_middle(sp, store_z1)
            for u in range(2):
                sp.wait_ge(z1_stored[u], 16 * (NCH // 2 - 1))
                sp.dma_start(z1_in[:, u, :], z1_dram[u, :, :]).then_inc(z1_loaded[u], 16)
            for g in range(NG):
                if g == 2:
                    sp.wait_ge(prodT_done, NCH)
                load_group(w2, 1, g)
            store_z1(NCH - 2, 0)
            store_z1(NCH - 1, 1)
            load_z1(2, 0)
            load_z1(3, 1)
            wait_split(sp, 1, NG - 1)
            full = (KT1 - 1) * P
            sp.dma_start(wt1_sb[:, 0:KT1 - 1, :], wt1[0:full, :].rearrange("(t p) n -> p t n", p=P)).then_inc(top_in, 16)
            sp.dma_start(wt1_sb[0:TOP_IN - full, KT1 - 1, :], wt1[full:TOP_IN, :]).then_inc(top_in, 16)
            sp.dma_start(wt2_sb, wt2.rearrange("(t p) n -> p t n", p=P)).then_inc(top_in, 16)
            for u in range(2):
                sp.wait_ge(z1_stored[u], 16 * NCH // 2)
            with sp.Fori(2, NCH // 2) as i:
                load_z1(2 * i, 0)
                load_z1(2 * i + 1, 1)
            sp.wait_ge(top_act, 7)
            sp.dma_start(out.rearrange("b a -> a b"), y_sb).then_inc(out_stored, 16)
            sp.wait_ge(out_stored, 16)

        @block.gpsimd
        def _(pool):
            nc.gpsimd.memset(ident[:], 0.0).then_inc(blank, 1)
            nc.gpsimd.memset(is_lo_row[:], 0.0).then_inc(blank, 1)
            nc.gpsimd.memset(is_rest_lo[:], 0.0).then_inc(blank, 1)
            pool.wait_ge(blank, 3)
            nc.gpsimd.affine_select(out=ident[:], in_=ident[:], compare_op=ALU.not_equal, fill=1.0, base=0,
                                    pattern=[[-1, P]], channel_multiplier=1).then_inc(consts, 1)
            nc.gpsimd.affine_select(out=is_lo_row[:], in_=is_lo_row[:], compare_op=ALU.is_ge, fill=1.0,
                                    base=GB - 1, pattern=[[0, 1]], channel_multiplier=-1).then_inc(consts, 1)
            nc.gpsimd.affine_select(out=is_rest_lo[:], in_=is_rest_lo[:], compare_op=ALU.is_ge, fill=1.0,
                                    base=2 * NREST - 1, pattern=[[0, 1]], channel_multiplier=-1).then_inc(consts, 1)

            def gather(b, f):
                nc.gpsimd.indirect_dma_start(
                    gath[:, b % 2, f, :], None, tables[f],
                    bass.IndirectOffsetOnAxis(ap=ids_sb[:, b, f:f + 1], axis=0)).then_inc(gathered[b], 16)

            def next_products(c, u, blocks):
                wait(pool, prodT_done, c - 1)
                pool.wait_ge(x0_block, 2 * blocks)
                products(nc.gpsimd, c, u).then_inc(prod_ready, 1)

            pool.wait_ge(ids_in, 16)
            for f in range(F):
                gather(0, f)
            pool.wait_ge(w0_done, 2)
            per_chunk = -(-F // (D - 3))
            for b in range(NBLK - 1):
                for d in range(D):
                    if b or d:
                        next_products(b * D + d, d % 2, b + 1)
                    for f in range(per_chunk * d, min(per_chunk * (d + 1), F)):
                        gather(b + 1, f)
                pool.wait_ge(gathered[b + 1], 16 * F)
                if b == 0:
                    wait_split(pool, 0, NG - 1)
                chunk_major(nc.gpsimd, b + 1, 0, D, x0_block)
            with pool.Fori(0, D // 2) as i:
                for u in range(2):
                    next_products((NBLK - 1) * D + 2 * i + u, u, NBLK)

            for g in range(NG):
                pool.wait_ge(w_hi_done, 2 * (NG + g) + 1)
                split_lo(nc.gpsimd, 1, g).then_inc(w_lo_done, 1)
                if stacks_by("pool", 1, g) > stacks_by("pool", 1, g - 1):
                    pool.wait_ge(w_hi_done, 2 * (NG + g) + 2)
                    split_stack(nc.gpsimd, 1, g).then_inc(w_st_pool, 1)

        @block.scalar
        def _(act):
            act.wait_ge(consts, 3)
            act.wait_ge(w0_sum, 2)
            a_raw = area[:, 0:(T0 + 1) * O].rearrange("p (t o) -> p t o", o=O)
            nc.scalar.activation(w0[:, :, 0, :], a_raw[:, 0:T0, :], ACT.Copy).then_inc(w0_hi_done, 1)
            nc.scalar.activation(w0_rest[:], a_raw[0:RREST, T0, :], ACT.Copy,
                                 scale=is_rest_lo[0:RREST, :]).then_inc(w0_hi_done, 1)

            def round_weights(layer, groups):
                for g in groups:
                    n = layer * NG + g
                    size = group_cols(g)
                    cols = slice(2 * g * O, 2 * g * O + size)
                    act.wait_ge(raw_in[n % NSLOT], 16 * 3 * (n // NSLOT + 1))
                    if layer:
                        act.wait_ge(y_done, w_released(g))
                    nc.scalar.activation(w_hi[:, cols], stage(layer, g)[:, 0, 0:size], ACT.Copy).then_inc(w_hi_done, 1)
                    nc.scalar.activation(w_st[0:RS, :, cols], stage(layer, g)[0:RS, 1:3, 0:size], ACT.Copy,
                                         scale=is_lo_row[0:RS, :]).then_inc(w_hi_done, 1)

            def hidden_hi(z, n):
                wait(act, hT_done, n)
                nc.scalar.activation(hs[:, 0:O], z, ACT.Relu).then_inc(hs_hi, 1)
                twice = hs[:].rearrange("p (a n) -> p a n", a=2)[:, :, O:O + GH]
                nc.scalar.activation(twice, z[:, GA:O].rearrange("p (a n) -> p a n", a=2), ACT.Relu).then_inc(hs_hi, 1)

            def hidden_T(n, u):
                act.wait_ge(hT_done, n + 1)
                wait(act, y_done, hT_free(n))
                nc.scalar.activation(hT[:, u, 0:2, :], hT_ps[:, 0:2, :], ACT.Copy).then_inc(hT_ready, 1)
                nc.scalar.activation(hT[0:RS, u, 2:4, :], hT_ps[0:RS, 2:4, :], ACT.Copy).then_inc(hT_ready, 1)

            def prepare1(c, u):
                if isinstance(c, int) and c == 0:
                    act.wait_ge(first_prod, 1)
                else:
                    act.wait_ge(prod_ready, c)
                wait(act, prodT_done, c)
                ends = rest[:].rearrange("p (a n) -> p a n", a=3)[:, 0:3:2, :]
                pairs = prod[:, u, T0 * P:NPAIR].unsqueeze(1).to_broadcast([P, 2, NREST])
                nc.scalar.activation(ends, pairs, ACT.Copy).then_inc(rest_hi, 1)
                act.wait_ge(prodT_done, c + 1)
                wait(act, z0_done, c)
                nc.scalar.activation(restT[:], prodT_ps[0:RREST, T0, :], ACT.Copy).then_inc(restT_done, 1)
                nc.scalar.activation(prodT_hi[:], prodT_ps[:, 0:T0, :], ACT.Copy).then_inc(prodT_hi_done, 1)
                act.wait_ge(z0_biased, c + 1)
                hidden_hi(z0_sb[:], c)
                hidden_T(c, u)

            def hidden2_hi(c, u):
                act.wait_ge(z1_loaded[u], z1_count(c, u))
                hidden_hi(z1_in[:, u, :], NCH + c)

            def prepare2(c, u):
                hidden2_hi(c, u)
                hidden_T(NCH + c, u)

            def z1_count(c, u):
                return 8 * (c - u) + 16

            round_weights(0, range(NG))
            for c in range(3):
                prepare1(c, c % 2)
            over_middle(act, lambda c, u: prepare1(c + 1, 1 - u))
            prepare1(NCH - 1, 1)
            hidden2_hi(0, 0)
            round_weights(1, range(0, 5))
            hidden2_hi(1, 1)
            round_weights(1, range(5, 8))
            hidden_T(NCH, 0)
            round_weights(1, range(8, 13))
            hidden_T(NCH + 1, 1)
            round_weights(1, range(13, NG))
            prepare2(2, 0)
            over_middle(act, lambda c, u: prepare2(c + 1, 1 - u))
            prepare2(NCH - 1, 1)

            act.wait_ge(top_in, 16 * 7)
            for t in range(KT1):
                rows = min(P, TOP_IN - t * P)
                act.wait_ge(xT_ps_done, t + 1)
                nc.scalar.activation(xT[0:rows, t, :], top_xT_ps(t)[0:rows, :], ACT.Copy).then_inc(xT_done, 1)
            for m in range(4):
                act.wait_ge(top_mm, m + 1)
                nc.scalar.activation(h1T[:, m, :], top1_ps(m), ACT.Relu, bias=bt1_sb[:, m:m + 1]).then_inc(top_act, 1)
            for m in range(2):
                act.wait_ge(top_mm, 5 + m)
                nc.scalar.activation(h2T[:, m, :], y_ps[:, m, :], ACT.Relu, bias=bt2_sb[:, m:m + 1]).then_inc(top_act, 1)
            act.wait_ge(top_mm, 7)
            nc.scalar.activation(y_sb, y_ps[0:1, 2, 0:B], ACT.Copy).then_inc(top_act, 1)

        @block.vector
        def _(dve):
            a_raw = area[:, 0:(T0 + 1) * O]
            b_raw = top_x[:].rearrange("p b n -> p (b n)")[:, 0:(T0 + 1) * O]
            nc.vector.memset(b_raw[:, 0:O], 0.0).then_inc(w0_blank, 1)
            dve.wait_ge(w0_in, 9 * 16)
            full = T0 * O
            nc.vector.tensor_tensor(a_raw[:, 0:full], a_raw[:, 0:full], b_raw[:, 0:full], ALU.add).then_inc(w0_sum, 1)
            nc.vector.tensor_tensor(a_raw[0:RREST, full:], a_raw[0:RREST, full:], b_raw[0:RREST, full:],
                                    ALU.add).then_inc(w0_sum, 1)
            dve.wait_ge(w0_sum, 2)
            nc.vector.memset(top_x[:], 0.0).then_inc(top_blank, 1)
            dve.wait_ge(w0_hi_done, 1)
            nc.vector.tensor_tensor(w0[:, :, 1, :], a_raw[:, 0:full].rearrange("p (t o) -> p t o", o=O),
                                    w0[:, :, 0, :].bitcast(f32), ALU.subtract).then_inc(w0_done, 1)
            dve.wait_ge(w0_hi_done, 2)
            nc.vector.tensor_tensor(w0_rest[:], a_raw[0:RREST, full:], w0_rest[:].bitcast(f32),
                                    ALU.subtract).then_inc(w0_done, 1)

            def rest_lo_part(c, u):
                dve.wait_ge(rest_hi, c + 1)
                nc.vector.tensor_tensor(rest[:, NREST:2 * NREST], prod[:, u, T0 * P:NPAIR],
                                        rest[:, 0:NREST].bitcast(f32), ALU.subtract).then_inc(rest_lo, 1)

            def prod_lo(c):
                dve.wait_ge(prodT_hi_done, c + 1)
                nc.vector.tensor_tensor(prodT_lo[:], prodT_ps[:, 0:T0, :], prodT_hi[:].bitcast(f32),
                                        ALU.subtract).then_inc(prodT_lo_done, 1)

            def z0_bias(c):
                dve.wait_ge(z0_done, c + 1)
                wait(dve, hs_hi, 2 * c)
                wait(dve, hs_lo, c)
                wait(dve, sums0, c)
                nc.vector.tensor_tensor(z0_sb[:], z0_ps[:, 0:O], bias[:, 0, :], ALU.add).then_inc(z0_part, 1)
                dve.wait_ge(z0_part, c + 1)
                nc.vector.tensor_tensor(z0_sb[:], z0_ps[:, O:2 * O], z0_sb[:], ALU.add).then_inc(z0_biased, 1)

            def hidden_lo(z, n):
                dve.wait_ge(hs_hi, 2 * n + 1)
                nc.vector.scalar_tensor_tensor(out=hs[:, O + GH:2 * O + GH], in0=z, scalar=0.0,
                                               in1=hs[:, 0:O].bitcast(f32), op0=ALU.max,
                                               op1=ALU.subtract).then_inc(hs_lo, 1)

            def add_to_sums(z, layer, c, s, count):
                to = top_x[:, c // D, layer * O:(layer + 1) * O]
                wait(dve, s, count)
                nc.vector.scalar_tensor_tensor(out=to, in0=z, scalar=0.0, in1=to, op0=ALU.max,
                                               op1=ALU.add).then_inc(s, 1)

            def hidden0_lo(c):
                dve.wait_ge(z0_biased, c + 1)
                hidden_lo(z0_sb[:], c)
                add_to_sums(z0_sb[:], 0, c, sums0, c)

            def hidden2_lo(c, u):
                dve.wait_ge(z1_loaded[u], z1_count(c, u))
                hidden_lo(z1_in[:, u, :], NCH + c)

            def take_x0(n, u):
                c = n % NCH if isinstance(n, int) else n
                if isinstance(n, int) and n < NCH:
                    dve.wait_ge(x0_block, 2 * (n // D + 1))
                wait(dve, z_done, n - 1)
                nc.vector.tensor_scalar(x0[:, u, :], x0_all[:, c, 0:F], 1.0, None, ALU.mult).then_inc(x0_ready, 1)

            def scale_unit(layer, n0, u0, order, pos, between):
                second, k = order[pos]
                n, u = n0 + second, (u0 + second) % 2
                done = summed_after(order)
                y = y_columns(2 * pos % NBANK, k)
                if k == 0:
                    dve.wait_ge(x0_ready, n + 1)
                    wait(dve, z_done, n - 1)
                for q in (0, 1):
                    dve.wait_ge(y_done, NY * n0 + 2 * pos + q + 1)
                    for f in unit_fields(k):
                        if group_of(f) % 2 != q:
                            continue
                        column = (f - UNIT * k) * O
                        part = y[:, column:column + O]
                        scale = x0[:, u, f:f + 1]
                        to = acc[:, u, f % 2, :]
                        if f == 1:
                            nc.vector.tensor_scalar(to, part, scale, None, ALU.mult).then_inc(summed, 1)
                        else:
                            if f:
                                dve.wait_ge(summed, F * n0 + done[second, f - 2])
                            nc.vector.scalar_tensor_tensor(
                                out=to, in0=part, scalar=scale, in1=to if f else bias[:, layer, :],
                                op0=ALU.mult, op1=ALU.add).then_inc(summed, 1)
                    if k == NU - 1 and q:
                        finish_z(layer, n, u, F * n0 + done[second, F - 1])
                    between(2 * pos + q)

            def finish_z(layer, n, u, done):
                c = n - (layer - 1) * NCH
                z = (z1_out if layer == 1 else z2_sb)[:, u, :]
                dve.wait_ge(summed, done)
                if layer == 1:
                    wait(dve, z1_stored[u], z1_count(c, u) - 16)
                wait(dve, sums12, n - 1)
                nc.vector.tensor_tensor(z, acc[:, u, 0, :], acc[:, u, 1, :], ALU.add).then_inc(z_done, 1)
                dve.wait_ge(z_done, n + 1)
                add_to_sums(z, layer, c, sums12, n)

            def z1_count(c, u):
                return 8 * (c - u) + 16

            def step1(c, u):
                def between(q):
                    if q == 0:
                        rest_lo_part(c + 1, 1 - u)
                    if q == 6:
                        prod_lo(c + 1)
                    if q == 9:
                        z0_bias(c + 1)
                    if q == 10:
                        hidden0_lo(c + 1)
                    if q == 12:
                        dve.wait_ge(prod_ready, c + 1)
                        take_x0(c + 1, 1 - u)
                for pos in range(NU):
                    scale_unit(1, c, u, ALONE, pos, between)

            def step2(c, u, last=False):
                n = NCH + c

                def between(q):
                    if last:
                        return
                    if q == 3:
                        hidden2_lo(c + 1, 1 - u)
                    if q == 12:
                        wait(dve, z_done, n)
                        nc.vector.tensor_scalar(x0[:, 1 - u, :], x0_all[:, c + 1, 0:F], 1.0, None,
                                                ALU.mult).then_inc(x0_ready, 1)
                for pos in range(NU):
                    scale_unit(2, n, u, ALONE, pos, between)

            def split_due(g):
                return 13 + 3 * g // 2

            def pair_step(layer, order, n, first, hooks):
                def between(q):
                    hooks(q)
                    for g in range(NG):
                        if split_due(g) == first + q and stacks_by("dve", 1, g) > stacks_by("dve", 1, g - 1):
                            dve.wait_ge(w_hi_done, 2 * (NG + g) + 2)
                            split_stack(nc.vector, 1, g).then_inc(w_st_dve, 1)
                for pos in range(len(order)):
                    scale_unit(layer, n, 0, order, pos, between)

            for g in range(NG):
                dve.wait_ge(w_hi_done, 2 * g + 1)
                split_lo(nc.vector, 0, g).then_inc(w_lo_done, 1)
                dve.wait_ge(w_hi_done, 2 * g + 2)
                split_stack(nc.vector, 0, g).then_inc(w_st_dve, 1)
            dve.wait_ge(gathered[0], 16 * F)
            chunk_major(nc.vector, 0, 0, 1, x0_first)
            dve.wait_ge(x0_first, 2)
            dve.wait_ge(w0_done, 2)
            products(nc.vector, 0, 0).then_inc(first_prod, 1)
            rest_lo_part(0, 0)
            chunk_major(nc.vector, 0, 1, D, x0_block)
            dve.wait_ge(bias_in, 16 * 3)
            prod_lo(0)
            take_x0(0, 0)
            z0_bias(0)
            hidden0_lo(0)
            step1(0, 0)
            step1(1, 1)
            over_middle(dve, step1)

            def between_closing(q):
                if q == 1:
                    prod_lo(NCH - 1)
                if q == 4:
                    z0_bias(NCH - 1)
                if q == 5:
                    hidden0_lo(NCH - 1)
                if q == 6:
                    take_x0(NCH - 1, 1)
                if q == 10:
                    hidden2_lo(0, 0)
                if q == 20:
                    hidden2_lo(1, 1)
                if q == 24:
                    take_x0(NCH, 0)

            def between_opening(q):
                if q == 1:
                    take_x0(NCH + 1, 1)
                if q == 15:
                    hidden2_lo(2, 0)
                if q == 27:
                    take_x0(NCH + 2, 0)

            rest_lo_part(NCH - 1, 1)
            pair_step(1, CLOSING, NCH - 2, 0, between_closing)
            pair_step(2, OPENING, NCH, 2 * NY, between_opening)
            over_middle(dve, step2)
            step2(NCH - 2, 0)
            step2(NCH - 1, 1, last=True)

        @block.tensor
        def _(pe):
            pe.wait_ge(consts, 1)

            def transpose(to, src):
                return nc.tensor.transpose(to, src, ident[:])

            def prod_T(c, u):
                if isinstance(c, int) and c == 0:
                    pe.wait_ge(first_prod, 1)
                else:
                    pe.wait_ge(prod_ready, c)
                pe.wait_ge(rest_lo, c + 1)
                wait(pe, prodT_lo_done, c)
                wait(pe, restT_done, c)
                for t in range(T0):
                    transpose(prodT_ps[:, t, :], prod[:, u, t * P:(t + 1) * P])
                transpose(prodT_ps[0:RREST, T0, :], rest[:].bitcast(f32)).then_inc(prodT_done, 1)

            def layer0(c):
                pe.wait_ge(prodT_lo_done, c + 1)
                wait(pe, z0_biased, c)
                pe.wait_ge(restT_done, c + 1)
                for t in range(T0):
                    nc.tensor.matmul(z0_ps[:, 0:2 * O], prodT_hi[:, t, :], w0[:, t, :, :], start=t == 0, stop=False)
                    nc.tensor.matmul(z0_ps[:, 0:O], prodT_lo[:, t, :], w0[:, t, 0, :], start=False, stop=False)
                nc.tensor.matmul(z0_ps[:, 0:O], restT[:], w0_rest[:], start=False, stop=True).then_inc(z0_done, 1)

            def hidden_T(n):
                pe.wait_ge(hs_hi, 2 * n + 2)
                pe.wait_ge(hs_lo, n + 1)
                wait(pe, hT_ready, 2 * n)
                src = hs[:].bitcast(f32)
                low = GA + RS
                transpose(hT_ps[:, 0, :], src[:, 0:GA])
                transpose(hT_ps[:, 1, :], src[:, low:low + GA])
                transpose(hT_ps[0:RS, 2, :], src[:, GA:low])
                transpose(hT_ps[0:RS, 3, :], src[:, low + GA:low + low]).then_inc(hT_done, 1)

            def unit_half(n0, u, order, q, layer_begins=None):
                _, k = order[q // 2]
                wait(pe, summed, bank_free(n0, order, q))
                size = half(k)
                first = UNIT * k * O + (q % 2) * size
                cols = slice(first, first + size)
                if layer_begins is not None:
                    wait_split(pe, layer_begins, (first + size - 1) // (2 * O))
                y = y_columns(q // 2 * 2 % NBANK, k)[:, (q % 2) * size:(q % 2 + 1) * size]
                nc.tensor.matmul(y, hT[:, u, 0, :], w_hi[:, cols], start=True, stop=False)
                nc.tensor.matmul(y, hT[:, u, 1, :], w_hi[:, cols], start=False, stop=False)
                nc.tensor.matmul(y, hT[:, u, 0, :], w_lo[:, cols], start=False, stop=False)
                nc.tensor.matmul(y, hT[0:RS, u, 2, :], w_st[0:RS, 0, cols], start=False, stop=False)
                nc.tensor.matmul(y, hT[0:RS, u, 3, :], w_st[0:RS, 1, cols], start=False, stop=True).then_inc(y_done, 1)

            def step1(c, u):
                pe.wait_ge(hT_ready, 2 * c + 2)
                for q in range(NY):
                    if q == 4:
                        prod_T(c + 1, 1 - u)
                    if q == 9:
                        layer0(c + 1)
                    if q == 14:
                        hidden_T(c + 1)
                    unit_half(c, u, ALONE, q, 0 if isinstance(c, int) and c == 0 else None)

            def top_transpose(t):
                rows = min(P, TOP_IN - t * P)
                for b in range(NBLK):
                    last = transpose(top_xT_ps(t)[0:rows, b * P:(b + 1) * P], top_x[:, b, t * P:t * P + rows])
                last.then_inc(xT_ps_done, 1)

            def top_layer1(tiles):
                for t in tiles:
                    rows = min(P, TOP_IN - t * P)
                    pe.wait_ge(xT_done, t + 1)
                    for m in range(4):
                        last = nc.tensor.matmul(top1_ps(m), wt1_sb[0:rows, t, m * P:(m + 1) * P], xT[0:rows, t, :],
                                                start=t == 0, stop=t == KT1 - 1)
                        if t == KT1 - 1:
                            last.then_inc(top_mm, 1)

            def step2(c, u, last=False):
                n = NCH + c
                pe.wait_ge(hT_ready, 2 * n + 2)
                for q in range(NY):
                    if q == 10 and not last:
                        hidden_T(n + 1)
                    if last and q == 8:
                        pe.wait_ge(sums0, NCH)
                        pe.wait_ge(sums12, NCH)
                        for t in range(3):
                            top_transpose(t)
                    unit_half(n, u, ALONE, q)

            prod_T(0, 0)
            pe.wait_ge(w0_done, 2)
            layer0(0)
            hidden_T(0)
            step1(0, 0)
            step1(1, 1)
            over_middle(pe, step1)
            for q in range(2 * NY):
                u, k = CLOSING[q // 2]
                if q == 1:
                    prod_T(NCH - 1, 1)
                if q == 4:
                    layer0(NCH - 1)
                if q == 8:
                    hidden_T(NCH - 1)
                if q == 16:
                    hidden_T(NCH)
                if q == 29:
                    hidden_T(NCH + 1)
                if k == 0:
                    pe.wait_ge(hT_ready, 2 * (NCH - 2 + u) + 2)
                unit_half(NCH - 2, u, CLOSING, q)
            for q in range(2 * NY):
                u, k = OPENING[q // 2]
                if q == 20:
                    hidden_T(NCH + 2)
                if k == 0:
                    pe.wait_ge(hT_ready, 2 * (NCH + u) + 2)
                unit_half(NCH, u, OPENING, q, 1 if u == 0 else None)
            over_middle(pe, step2)
            step2(NCH - 2, 0)
            step2(NCH - 1, 1, last=True)

            pe.wait_ge(top_in, 16 * 7)
            pe.wait_ge(xT_done, 3)
            top_layer1([0, 1])
            pe.wait_ge(sums12, 2 * NCH)
            top_transpose(3)
            top_transpose(4)
            top_layer1([2, 3, 4])
            for m in range(2):
                for t in range(4):
                    if m == 0:
                        pe.wait_ge(top_act, t + 1)
                    if t == 0:
                        pe.wait_ge(xT_done, KT1)
                    last = nc.tensor.matmul(y_ps[:, m, :], wt2_sb[:, t, m * P:(m + 1) * P], h1T[:, t, :],
                                            start=t == 0, stop=t == 3)
                last.then_inc(top_mm, 1)
            for t in range(2):
                pe.wait_ge(top_act, 5 + t)
                last = nc.tensor.matmul(y_ps[0:1, 2, 0:B], wt3_sb[:, t:t + 1], h2T[:, t, :], start=t == 0, stop=t == 1)
            last.then_inc(top_mm, 1)


def kernel(**inputs):
    import numpy as np
    import concourse.bacc as bacc
    from concourse import mybir as mb
    from concourse.bass_utils import run_bass_kernel_spmd as run

    nc = bacc.Bacc("TRN2", target_bir_lowering=False, num_devices=1)
    arrays = {}

    def given(name, a):
        a = np.ascontiguousarray(a)
        arrays[name] = a
        return nc.dram_tensor(name, a.shape, mb.dt.from_np(a.dtype), kind="ExternalInput").ap()

    ids = given("ids_dram", inputs["ids"])
    tables = [given(f"tbl_{f}_dram", inputs[f"tbl_{f}"]) for f in range(F)]
    dense = given("dense_dram", inputs["dense_ctx"])
    f = np.tile(np.arange(F), K2)
    g = (f + np.repeat(np.arange(K2), F)) % F
    w0 = np.asarray(inputs["L0_rec_W0"])
    w0_a = given("w0_a_dram", w0[:, f, g].T)
    w0_b = given("w0_b_dram", w0[:, g[F:], f[F:]].T)
    w1, w2 = (given(f"w{n}_dram", np.asarray(inputs[f"L0_rec_W{n}"]).transpose(2, 1, 0).reshape(O, F * O)) for n in (1, 2))
    b = [given(f"b{n}_dram", inputs[f"L0_rec_b{n}"]) for n in range(3)]
    wt1 = given("wt1_dram", inputs["W_top1"])
    bt1 = given("bt1_dram", np.asarray(inputs["b_top1"]).reshape(4, P).T)
    wt2 = given("wt2_dram", inputs["W_top2"])
    bt2 = given("bt2_dram", np.asarray(inputs["b_top2"]).reshape(2, P).T)
    wt3 = given("wt3_dram", np.asarray(inputs["W_top3"]).reshape(2, P).T)
    out = nc.dram_tensor("y_dram", (B, 1), mb.dt.float32, kind="ExternalOutput").ap()
    dlrm_tower(nc, ids, tables, dense, w0_a, w0_b, w1, w2, *b, wt1, bt1, wt2, bt2, wt3, out)
    return run(nc, [arrays], core_ids=[0]).results[0]["y_dram"]
```
